# Optimizing a Trainium2 kernel written in Bass

```python
import numpy as np
import jax
import jax.numpy as jnp

def _softmax(x, axis=-1):
    return jax.nn.softmax(x, axis=axis)

def _gelu(x):
    return jax.nn.gelu(x, approximate=True)

def _silu(x):
    return jax.nn.silu(x)

def _sigmoid(x):
    return jax.nn.sigmoid(x)

def _layernorm(x, axis=-1, eps=1e-05):
    m = jnp.mean(x, axis=axis, keepdims=True)
    v = jnp.var(x, axis=axis, keepdims=True)
    return (x - m) / jnp.sqrt(v + eps)

def _scatter_add(tgt, idx, src, axis=0):
    return tgt.at[idx].add(src)

def _segment_sum(src, seg, n):
    return jax.ops.segment_sum(src, seg, n)
kernel_name = 'mk_gnn_resnorm_d4_gnn_r64_c321eb'

def setup_inputs(seed: int=0):
    np.random.seed(seed)
    _w = jnp.asarray

    def _rec_inputs():
        import jax
        import jax.numpy as jnp
        _gk = jax.random.key(seed)
        x = -0.0001006 + 1 * jax.random.normal(jax.random.fold_in(_gk, 1), (100000, 48), jnp.float32)
        src = jax.random.randint(jax.random.fold_in(_gk, 2), (25000,), 0, 100000, jnp.int32)
        dst = jax.random.randint(jax.random.fold_in(_gk, 3), (25000,), 0, 100000, jnp.int32)
        _o = jnp.argsort(dst, stable=True)
        src = src[_o]
        dst = dst[_o]
        edge_attr_40 = jax.random.uniform(jax.random.fold_in(_gk, 13), (25000, 40), jnp.float32, 0.0, 1)
        edge_weight = jax.random.uniform(jax.random.fold_in(_gk, 15), (25000,), jnp.float32, 0.0, 0.999999)
        node_type_119 = jax.random.randint(jax.random.fold_in(_gk, 16), (100000,), 0, 119, jnp.int32)
        node_vec = jax.random.uniform(jax.random.fold_in(_gk, 17), (100000,), jnp.float32, 0.0, 1.49999)
        return (x, src, dst, edge_attr_40, edge_weight, node_type_119, node_vec)
    x, src, dst, edge_attr_40, edge_weight, node_type_119, node_vec = _rec_inputs()

    def _L0_gnn_setup():
        import jax, jax.numpy as jnp
        import numpy as np
        NUM_NODES = 100000
        key = jax.random.key(seed)
        k1, k2, k3 = jax.random.split(key, 3)
        x = jax.random.normal(k1, (NUM_NODES, 48), dtype=jnp.float32)
        edge_index = jax.random.randint(k2, (2, 25000), 0, NUM_NODES, dtype=jnp.int64)
        edge_weight = jax.random.uniform(k3, (25000,), dtype=jnp.float32)
        return {'x': x, 'edge_index': edge_index, 'edge_weight': edge_weight}
    _L0_gnn_all = _L0_gnn_setup()
    _L0_gnn_in = {k: v for k, v in _L0_gnn_all.items() if k in ()}
    del _L0_gnn_all

    def _L1_gnn_setup():
        import jax, jax.numpy as jnp
        import numpy as np
        CUTOFF = 6.0
        LN_EPS = 1e-05
        key = jax.random.key(seed)
        ks = jax.random.split(key, 16)
        N, E, H, R, NEL, G = (50000, 12500, 48, 40, 119, 32)
        inp = {'h': jax.random.normal(ks[0], (N, H), jnp.float32), 'edge_index': jax.random.randint(ks[1], (2, E), 0, N, jnp.int64), 'edge_attr': jax.random.uniform(ks[2], (E, R), jnp.float32), 'distances': jax.random.uniform(ks[3], (E,), jnp.float32) * 7.0, 'atom_z': jax.random.randint(ks[4], (N,), 0, NEL, jnp.int64), 'node_mult': jax.random.uniform(ks[5], (N,), jnp.float32) + 0.5, 'batch': jnp.zeros((N,), jnp.int64), 'W1': jax.random.normal(ks[6], (H, R), jnp.float32) / np.sqrt(R), 'b1': jax.random.normal(ks[7], (H,), jnp.float32) * 0.01, 'W2': jax.random.normal(ks[8], (H, H), jnp.float32) / np.sqrt(H), 'b2': jax.random.normal(ks[9], (H,), jnp.float32) * 0.01, 'emb': jax.random.normal(ks[10], (NEL, G), jnp.float32) * 0.01, 'adaptW': jax.random.normal(ks[11], (G, G), jnp.float32) * 0.01, 'gamma': jnp.ones((H,), jnp.float32), 'beta': jnp.zeros((H,), jnp.float32)}
        return inp
    _L1_gnn_all = _L1_gnn_setup()
    _L1_gnn_in = {k: v for k, v in _L1_gnn_all.items() if k in ('W1', 'b1', 'W2', 'b2', 'emb', 'adaptW', 'gamma', 'beta')}
    del _L1_gnn_all

    def _L2_gnn_setup():
        import jax, jax.numpy as jnp
        import numpy as np
        N_NODES = 100000
        N_EDGES = 25000
        D_IN = 48
        D_OUT = 48
        key = jax.random.key(seed)
        k1, k2, k3, k4, k5, k6 = jax.random.split(key, 6)
        inputs = jax.random.normal(k1, (N_NODES, D_IN), dtype=jnp.float32)
        edge_row = jnp.sort(jax.random.randint(k2, (N_EDGES,), 0, N_NODES, dtype=jnp.int64))
        edge_col = jax.random.randint(k3, (N_EDGES,), 0, N_NODES, dtype=jnp.int64)
        edge_val = jax.random.uniform(k4, (N_EDGES,), dtype=jnp.float32)
        std = float(np.sqrt(2.0 / (D_IN + D_OUT)))
        weight = jax.random.normal(k5, (D_IN, D_OUT), dtype=jnp.float32) * std
        bias = jnp.zeros((D_OUT,), dtype=jnp.float32)
        return {'inputs': inputs, 'edge_row': edge_row, 'edge_col': edge_col, 'edge_val': edge_val, 'weight': weight, 'bias': bias}
    _L2_gnn_all = _L2_gnn_setup()
    _L2_gnn_in = {k: v for k, v in _L2_gnn_all.items() if k in ('weight', 'bias')}
    del _L2_gnn_all

    def _L3_gnn_setup():
        import jax, jax.numpy as jnp
        import numpy as np
        N_NODES = 100000
        N_EDGES = 25000
        C_IN = 48
        C_OUT = 48
        key = jax.random.key(seed)
        k_x, k_e, k_w = jax.random.split(key, 3)
        x = jax.random.normal(k_x, (N_NODES, C_IN), dtype=jnp.float32)
        edge_index = jax.random.randint(k_e, (2, N_EDGES), 0, N_NODES, dtype=jnp.int64)
        W = jax.random.normal(k_w, (C_IN, C_OUT), dtype=jnp.float32) * (1.0 / np.sqrt(C_IN))
        b = jnp.zeros((C_OUT,), dtype=jnp.float32)
        return {'x': x, 'edge_index': edge_index, 'W': W, 'b': b}
    _L3_gnn_all = _L3_gnn_setup()
    _L3_gnn_in = {k: v for k, v in _L3_gnn_all.items() if k in ('W', 'b')}
    del _L3_gnn_all
    return {'x': x, 'src': src, 'dst': dst, 'edge_attr_40': edge_attr_40, 'edge_weight': edge_weight, 'node_type_119': node_type_119, 'node_vec': node_vec, 'L1_gnn_W1': _L1_gnn_in['W1'], 'L1_gnn_b1': _L1_gnn_in['b1'], 'L1_gnn_W2': _L1_gnn_in['W2'], 'L1_gnn_b2': _L1_gnn_in['b2'], 'L1_gnn_emb': _L1_gnn_in['emb'], 'L1_gnn_adaptW': _L1_gnn_in['adaptW'], 'L1_gnn_gamma': _L1_gnn_in['gamma'], 'L1_gnn_beta': _L1_gnn_in['beta'], 'L2_gnn_weight': _L2_gnn_in['weight'], 'L2_gnn_bias': _L2_gnn_in['bias'], 'L3_gnn_W': _L3_gnn_in['W'], 'L3_gnn_b': _L3_gnn_in['b']}

def reference(x, src, dst, edge_attr_40, edge_weight, node_type_119, node_vec, L1_gnn_W1, L1_gnn_b1, L1_gnn_W2, L1_gnn_b2, L1_gnn_emb, L1_gnn_adaptW, L1_gnn_gamma, L1_gnn_beta, L2_gnn_weight, L2_gnn_bias, L3_gnn_W, L3_gnn_b):
    import jax
    import jax.numpy as jnp

    def _L0_gnn_ref(x, edge_index, edge_weight):
        import jax, jax.numpy as jnp
        import numpy as np
        NUM_NODES = 100000
        src, dst = (edge_index[0], edge_index[1])
        msgs = x[src] * edge_weight[:, None]
        out = jax.ops.segment_sum(msgs, dst, num_segments=NUM_NODES)
        return out

    def _L1_gnn_ref(h, edge_index, edge_attr, distances, atom_z, node_mult, batch, W1, b1, W2, b2, emb, adaptW, gamma, beta):
        import jax, jax.numpy as jnp
        import numpy as np
        CUTOFF = 6.0
        LN_EPS = 1e-05
        src, dst = (edge_index[0], edge_index[1])
        N = h.shape[0]
        gate = jax.nn.silu(edge_attr @ W1.T + b1) @ W2.T + b2
        ei = emb[atom_z[src]]
        ej = emb[atom_z[dst]]
        adapt_logit = jnp.sum(ei * (ej @ adaptW.T), axis=-1, keepdims=True)
        gate = gate + adapt_logit
        cw = jnp.where(distances < CUTOFF, 0.5 * (jnp.cos(jnp.pi * distances / CUTOFF) + 1.0), 0.0)
        mj = node_mult[dst]
        msg = gate * h[dst] * (cw * mj)[:, None]
        agg = jax.ops.segment_sum(msg, src, num_segments=N)
        tot = jax.ops.segment_sum(mj, src, num_segments=N)
        agg = agg / jnp.clip(tot, 1e-08, None)[:, None]
        x = h + agg
        mu = jnp.mean(x, axis=-1, keepdims=True)
        var = jnp.mean(jnp.square(x - mu), axis=-1, keepdims=True)
        return (x - mu) / jnp.sqrt(var + LN_EPS) * gamma + beta

    def _L2_gnn_ref(inputs, edge_row, edge_col, edge_val, weight, bias):
        import jax, jax.numpy as jnp
        import numpy as np
        N_NODES = 100000
        N_EDGES = 25000
        D_IN = 48
        D_OUT = 48
        msgs = edge_val[:, None] * inputs[edge_col]
        agg = jax.ops.segment_sum(msgs, edge_row, num_segments=N_NODES)
        return agg @ weight + bias

    def _L3_gnn_ref(x, edge_index, W, b):
        import jax, jax.numpy as jnp
        import numpy as np
        N_NODES = 100000
        N_EDGES = 25000
        C_IN = 48
        C_OUT = 48
        N = x.shape[0]
        loops = jnp.arange(N, dtype=edge_index.dtype)
        src = jnp.concatenate([edge_index[0], loops])
        dst = jnp.concatenate([edge_index[1], loops])
        deg = jax.ops.segment_sum(jnp.ones(src.shape, dtype=x.dtype), dst, num_segments=N)
        dinv = jnp.where(deg > 0, jax.lax.rsqrt(deg), 0.0)
        norm = dinv[src] * dinv[dst]
        h = x @ W
        msg = h[src] * norm[:, None]
        out = jax.ops.segment_sum(msg, dst, num_segments=N)
        return out + b
    edge_index = jnp.stack([src, dst])
    batch0 = jnp.zeros((100000,), jnp.int32)
    x = _layernorm(x + _L0_gnn_ref(x, edge_index, edge_weight), axis=-1)
    x = _layernorm(x + _L1_gnn_ref(x, edge_index, edge_attr_40, edge_weight, node_type_119, node_vec, batch0, L1_gnn_W1, L1_gnn_b1, L1_gnn_W2, L1_gnn_b2, L1_gnn_emb, L1_gnn_adaptW, L1_gnn_gamma, L1_gnn_beta), axis=-1)
    x = _layernorm(x + _L2_gnn_ref(x, src, dst, edge_weight, L2_gnn_weight, L2_gnn_bias), axis=-1)
    x = _layernorm(x + _L3_gnn_ref(x, edge_index, L3_gnn_W, L3_gnn_b), axis=-1)
    return x

_drawn_inputs = setup_inputs


def setup_inputs(seed=0):
    import zlib

    import numpy as np

    out = dict(_drawn_inputs(seed))
    spreads = {'L1_gnn_gamma': (1.0, 0.2),
     'L1_gnn_beta': (0.0, 0.1),
     'L2_gnn_bias': (0.0, 0.1),
     'L3_gnn_b': (0.0, 0.1)}
    factors = {'node_vec': 60.682,
     'L1_gnn_b1': 41.931,
     'L1_gnn_b2': 26.089,
     'L1_gnn_emb': 64.0,
     'L1_gnn_adaptW': 64.0,
     'edge_attr_40': 3.23}
    for name, (base, spread) in spreads.items():
        noise = np.random.default_rng([zlib.crc32(name.encode()), seed]).standard_normal(out[name].shape)
        drawn = base * np.exp(spread * noise) if base else spread * noise
        out[name] = jnp.asarray(drawn.astype(out[name].dtype))
    for name, factor in factors.items():
        out[name] = (out[name] * factor).astype(out[name].dtype)
    return out
```

```python
import math
from contextlib import ExitStack, contextmanager

import concourse.bass as bass
from concourse import mybir

P = 128
N, E, D = 100000, 25000, 48
R, TYPES, EMB = 40, 119, 32
BATCH = 14
GROUP = 4
PAIRS = BATCH // 2
TILES = 196
CHUNKS = 28
C = 28
NODES = P * CHUNKS * C
EDGES = TILES * P
DUMP = GROUP * P
ROWS = NODES + DUMP
TRIPS = 7
BATCHES, GROUPS = 2, TILES // GROUP // TRIPS
EPS = 1e-5
DEG, MULT, TYPE, W0 = D, D + 1, D + 2, D + 4
AGG, TOT, W1 = D + 1, 2 * D + 1, 2 * D + 2
W2 = 2 * D + 1
HALF = PAIRS

assert TILES == TRIPS * BATCHES * BATCH == TRIPS * GROUPS * GROUP and EDGES >= E
assert NODES >= N + EDGES - E

START, START_DMA = 1, 16
TO_SRC = (0, 1, 1, 0)
PER_GATHER = (49, 18, 48, 18)
PER_SCATTER = (0, 2, 24, 8)
PER_LAST = 4

BULK_PARTS = {1: ["centre", "var", "norm"],
              2: ["centre", "var", "norm", "var2", "norm2"],
              3: ["centre", "var", "norm", "mm0", "mm1"]}
EDGE_PARTS = {0: ["message"],
              1: ["centre", "onehot0", "var", "logit0", "onehot1", "norm", "logit1", "message"],
              2: ["centre", "var", "norm", "var2", "message"],
              3: ["centre", "var", "message"]}


def mixed(a, b):
    keyed = [((k + 0.5) / len(a), 0, x) for k, x in enumerate(a)] + [((k + 0.5) / len(b), 1, x) for k, x in enumerate(b)]
    return [x for _, _, x in sorted(keyed, key=lambda y: y[:2])]


def gather_order(layer):
    out = []
    for u in range(BATCHES):
        if layer == 3:
            out += [("bulk", u, "centre"), ("edge", u, "centre"), ("bulk", u, "var"), ("edge", u, "var"),
                    ("edge", u, "message"), ("bulk", u, "norm"), ("bulk", u, "mm0"), ("bulk", u, "mm1")]
            continue
        bulk = [("bulk", u, x) for x in BULK_PARTS[layer]] if layer else []
        out += mixed([("edge", u, x) for x in EDGE_PARTS[layer]], bulk)
    return out


def scatter_order(layer):
    bulk = [("bulk", u, x) for u in range(2) for x in BULK_PARTS[layer]] if layer else []
    return mixed([("group", v, None) for v in range(GROUPS)], bulk)


def graph_layers(nc, x, node_mult, node_type, src_rows, dst_rows, src_tiles, dst_tiles, attr_t, weight_tiles,
                 w1_t, b1, w2_t, b2, emb, emb_t, adapt_t, gamma, beta, weight2, bias2, weight3, bias3, out):
    f32, i32 = mybir.dt.float32, mybir.dt.int32
    ALU, ACT, AX = mybir.AluOpType, mybir.ActivationFunctionType, mybir.AxisListType

    table0 = nc.dram_tensor("table0", [ROWS, W0], f32, kind="Internal").ap()
    table1 = nc.dram_tensor("table1", [ROWS, W1], f32, kind="Internal").ap()
    table2 = nc.dram_tensor("table2", [ROWS, W2], f32, kind="Internal").ap()
    base3 = nc.dram_tensor("base3", [NODES, D], f32, kind="Internal").ap()
    agg3 = nc.dram_tensor("agg3", [ROWS, D], f32, kind="Internal").ap()

    def by_chunk(t):
        return t[0:NODES, :].rearrange("(p c) w -> p c w", p=P)

    x_c, table0_c, table1_c, table2_c = by_chunk(x), by_chunk(table0), by_chunk(table1), by_chunk(table2)
    base3_c, agg3_c, out_c = by_chunk(base3), by_chunk(agg3), by_chunk(out)

    ctx = ExitStack()
    with ctx:
        def sb(name, shape, dt=f32):
            return ctx.enter_context(nc.sbuf_tensor(name, shape, dt))

        def sem(name):
            return ctx.enter_context(nc.semaphore(name))

        def pair(name):
            return [sem(f"{name}_{u}") for u in range(2)]

        ident = sb("ident", [P, P])
        earlier = sb("earlier", [P, DUMP + P])
        type_iota = sb("type_iota", [P, TYPES])
        dump_row = sb("dump_row", [P, TILES])
        zeros = sb("zeros", [P, W1])
        eps = sb("eps", [P, 1])
        half_pi = sb("half_pi", [P, 1])
        zero1 = sb("zero1", [P, 1])
        gamma_b = sb("gamma_b", [P, D])
        beta_b = sb("beta_b", [P, D])
        bias2_b = sb("bias2_b", [P, D])
        bias3_b = sb("bias3_b", [P, D])
        w1_sb = sb("w1_sb", [R, D])
        b1_sb = sb("b1_sb", [D, 1])
        w2_sb = sb("w2_sb", [D + 1, D])
        emb_sb = sb("emb_sb", [TYPES, EMB])
        embt_sb = sb("embt_sb", [EMB, TYPES])
        adapt_sb = sb("adapt_sb", [EMB, EMB])
        adapted = sb("adapted", [TYPES, EMB])
        wide2 = sb("wide2", [2 * D, 2 * D])
        wide3 = sb("wide3", [2 * D, 2 * D])
        src_i = sb("src_i", [P, TILES], i32)
        dst_i = sb("dst_i", [P, TILES], i32)
        src_f = sb("src_f", [P, TILES])
        dst_f = sb("dst_f", [P, TILES])
        ew = sb("ew", [P, TILES])
        cw = sb("cw", [P, TILES])
        src_seen = sb("src_seen", [P, TILES])
        dst_seen = sb("dst_seen", [P, TILES])
        src_to = sb("src_to", [P, TILES], i32)
        dst_to = sb("dst_to", [P, TILES], i32)
        src_type = sb("src_type", [P, TILES])
        dst_deg = sb("dst_deg", [P, TILES])
        msg = sb("msg", [P, TILES, D + 1])
        gate = sb("gate", [P, TILES, D])
        mult_in = msg[:, 0:16, :].rearrange("p t d -> p (t d)")[:, 0:CHUNKS * C]
        type_in = msg[:, 16:32, :].rearrange("p t d -> p (t d)")[:, 0:CHUNKS * C].bitcast(i32)
        rows = sb("rows", [P, 2, BATCH * W1])
        row_index = sb("row_index", [P, 2, BATCH], i32)
        edev = sb("edev", [P, BATCH, D])
        esq = sb("esq", [P, BATCH, D])
        esum = sb("esum", [P, BATCH])
        evar = sb("evar", [P, BATCH])
        estd = sb("estd", [P, BATCH])
        efac = sb("efac", [P, BATCH])
        efac2 = sb("efac2", [P, BATCH])
        logit = sb("logit", [P, BATCH])
        onehot = sb("onehot", [P, 2, HALF, TYPES])
        ej = sb("ej", [P, HALF, EMB])
        eij = sb("eij", [P, HALF, EMB])
        turned = sb("turned", [P, PAIRS * P])
        keyrow = sb("keyrow", [P, 2, 2, DUMP], i32)
        same = sb("same", [P, 2, GROUP, DUMP])
        to_add = sb("to_add", [P, 2, GROUP * (D + 1)])
        to_index = sb("to_index", [P, 2, GROUP], i32)
        bin_ = sb("bin", [P, 2, C * W1])
        bout = sb("bout", [P, 2, C * W0])
        bdev = sb("bdev", [P, C, D])
        bsq = sb("bsq", [P, C, D])
        bsum = sb("bsum", [P, C])
        bvar = sb("bvar", [P, C])
        bstd = sb("bstd", [P, C])
        bfac = sb("bfac", [P, C])
        attr_sb = [bin_[0:R, u, 0:HALF * P] for u in range(2)]
        hidden = bdev[0:64, :, :].rearrange("p c d -> p (c d)")[:, 0:HALF * P]
        seen_tmp = esq[:, :, :].rearrange("p b d -> p (b d)")

        ps = ctx.enter_context(nc.psum_tensor("ps", [P, 8, 512], f32))
        flat = ps[:, :, :].rearrange("p b n -> p (b n)")
        ps_turn = flat[:, 0:1024]
        ps_prod = flat[:, 1024:2048]
        ps_sum = [ps[:, 4, :], ps[:, 5, :]]
        ps_gate = [ps[:, 6, :], ps[:, 7, :]]

        s_const = sem("const_loaded")
        s_built = sem("const_built")
        s_iota = sem("iota_made")
        s_pool = sem("pool_step")
        s_ready = sem("edge_arrays_ready")
        s_adapt = sem("adapted_product")
        s_adapted = sem("adapted_ready")
        bulk_in, bulk_in2 = pair("bulk_loaded"), pair("bulk_loaded_sum")
        bulk_used, bulk_out, bulk_stored = pair("bulk_used"), pair("bulk_ready"), pair("bulk_stored")
        attr_in = pair("attr_loaded")
        s_hpre, s_hid = sem("hidden_product"), sem("hidden_ready")
        s_gpre, s_gate = sem("gate_product"), sem("gate_ready")
        s_zero = [sem(f"sums_zeroed_{k}") for k in range(4)]
        key_in, rows_in, rows_used, index_in = pair("keyrow_loaded"), pair("rows_gathered"), pair("rows_used"), pair("index_staged")
        s_counted = sem("keys_counted")
        s_same, s_summed, s_staged, s_added = sem("same_ready"), sem("sum_product"), sem("sum_staged"), sem("group_added")
        e_dev, e_sqd, e_var, e_std = sem("edge_centred"), sem("edge_squared"), sem("edge_variance"), sem("edge_deviation")
        s_deg, s_degroot = sem("degree_product"), sem("degree_root")
        b_dev, b_sqd, b_var, b_std = sem("bulk_centred"), sem("bulk_squared"), sem("bulk_variance"), sem("bulk_deviation")
        s_step = sem("vector_step")
        s_hot, s_hott, s_hotc = sem("onehot_ready"), sem("onehot_turned"), sem("onehot_turned_copied")
        s_look, s_ej, s_lookused = sem("types_looked_up"), sem("ej_copied"), sem("lookup_used")
        s_mmin, s_turned, s_turnc = sem("product_input"), sem("input_turned"), sem("input_turned_copied")
        s_prod, s_produsd = sem("product_ready"), sem("product_used")

        block = ctx.enter_context(nc.Block())

        BULK_TRIPS = 2 * TRIPS

        def apart(engine):
            engine.nop(nofuse=True)

        @block.sync
        def _(sync):
            n = [0]

            def const(to, of):
                sync.dma_start(to, of).then_inc(s_const, 16)
                n[0] += 1

            for started in (*bulk_used, *rows_used, s_counted, s_hpre, s_same, s_staged, s_summed, s_hid, s_gate, s_gpre,
                            s_hott, s_hotc, s_look, s_lookused, s_turned, s_produsd):
                sync.sem_inc(started, START)
            sync.dma_start(mult_in, node_mult.rearrange("(p c) -> p c", p=P)).then_inc(bulk_stored[0], 16)
            sync.dma_start(type_in, node_type.rearrange("(p c) -> p c", p=P)).then_inc(bulk_stored[1], 16)
            with sync.Fori(0, BULK_TRIPS) as i:
                for u in range(2):
                    sync.wait_ge(bulk_used[u], i + START)
                    sync.dma_start(bin_[:, u, 0:C * D].rearrange("p (c d) -> p c d", d=D),
                                   x_c[:, bass.ds((2 * i + u) * C, C), :]).then_inc(bulk_in[u], 16)
            sync.wait_ge(s_built, 1)
            const(src_i[:, :], src_tiles)
            const(dst_i[:, :], dst_tiles)
            const(ew[:, :], weight_tiles)
            for to, of in ((gamma_b, gamma), (beta_b, beta), (bias2_b, bias2), (bias3_b, bias3)):
                const(to[:, :], of.rearrange("(a d) -> a d", a=1).to_broadcast([P, D]))
            const(w1_sb[:, :], w1_t)
            const(b1_sb[:, :], b1.rearrange("(d a) -> d a", a=1))
            const(w2_sb[0:D, :], w2_t)
            const(w2_sb[D:D + 1, :], b2.rearrange("(a d) -> a d", a=1))
            const(emb_sb[:, :], emb)
            const(embt_sb[:, :], emb_t)
            const(adapt_sb[:, :], adapt_t)
            for to, of in ((wide2, weight2), (wide3, weight3)):
                for k in range(2):
                    const(to[k * D:k * D + D, k * D:k * D + D], of)
            assert n[0] == 18
            def zero(k, i, n, table, first, width):
                z = zeros[:, 0:width].rearrange("p (a w) -> p a w", a=1)
                for j in range(n):
                    sync.dma_start(by_chunk(table)[:, bass.ds((n * i + j) * C, C), first:first + width],
                                   z.to_broadcast([P, C, width])).then_inc(s_zero[k], 16)

            def zero_dump(k, table, first, width):
                sync.dma_start(table[NODES:ROWS, first:first + width].rearrange("(p c) w -> p c w", p=P),
                               zeros[:, 0:width].rearrange("p (a w) -> p a w", a=1).to_broadcast([P, DUMP // P, width]))\
                    .then_inc(s_zero[k], 16)

            def keyrows(g, v, which):
                for k in which:
                    sync.dma_start(keyrow[:, v % 2, k, :],
                                   (dst_rows, src_rows)[k][:, bass.ds(g * DUMP, DUMP)].to_broadcast([P, DUMP]))\
                        .then_inc(key_in[v % 2], 16)

            for u in range(2):
                sync.wait_ge(bulk_used[u], BULK_TRIPS + START)

            for layer in range(4):
                bulk = BULK_TRIPS * layer
                if layer == 1:
                    sync.wait_ge(s_added, 16 * TILES * layer + START_DMA)
                elif layer > 1:
                    sync.wait_ge(s_added, 16 * TILES * layer + START_DMA)
                    for u in range(2):
                        sync.wait_ge(bulk_stored[u], 16 * bulk + START_DMA)

                def chunk(q, u, ii):
                    table = (None, table0_c, table1_c, table2_c)[layer]
                    width = (0, W0, W1, W2)[layer]
                    sync.wait_ge(bulk_used[u], bulk + ii + START)
                    sync.dma_start(bin_[:, u, 0:C * width].rearrange("p (c w) -> p c w", w=width),
                                   table[:, bass.ds(q * C, C), :]).then_inc(bulk_in[u], 16)

                def store(q, u, ii):
                    sync.wait_ge(bulk_out[u], bulk + ii + 1)
                    width = (0, D + 1, D + 1, D)[layer]
                    to = (None, table1_c, table2_c, base3_c)[layer]
                    sync.dma_start(to[:, bass.ds(q * C, C), 0:width],
                                   bout[:, u, 0:C * width].rearrange("p (c w) -> p c w", w=width))\
                        .then_inc(bulk_stored[u], 16)

                cleared = ((table1, AGG, D + 1), (table2, AGG, D), (agg3, 0, D), None)[layer]
                with sync.Fori(0, TRIPS) as i:
                    if layer == 0:
                        for v in range(GROUPS):
                            g = GROUPS * i + v
                            sync.wait_ge(s_counted, (g - 1 if v else g) + START)
                            keyrows(g, v, (0, 1))
                            if v % 2 == 0:
                                j = 4 * i + v // 2
                                sync.wait_ge(s_hpre, (j - 1 if v else j) + START)
                                sync.dma_start(attr_sb[v // 2 % 2], attr_t[:, bass.ds(j * (HALF * P), HALF * P)])\
                                    .then_inc(attr_in[v // 2 % 2], 16)
                    else:
                        for u in range(2):
                            chunk(2 * i + u, u, i)
                            store(2 * i + u, u, i)
                    if cleared:
                        zero(layer + 1, i, CHUNKS // TRIPS, *cleared)
                if cleared:
                    zero_dump(layer + 1, cleared[0], 0, (W1, W2, D)[layer])
                if layer == 0:
                    sync.wait_ge(s_counted, GROUPS * TRIPS + START)
                    sync.wait_ge(s_hpre, TILES // HALF + START)
                with sync.Fori(0, TRIPS) as i:
                    for kind, k, part in scatter_order(layer):
                        if kind == "group":
                            g = GROUPS * i + k
                            sync.wait_ge(s_same, (GROUPS * TRIPS * layer + (g - 1 if k else g)) + START)
                            keyrows(g, k, (TO_SRC[layer],))
                        elif part == "centre":
                            chunk(BULK_TRIPS + 2 * i + k, k, TRIPS + i)
                            if k:
                                store(BULK_TRIPS + 2 * i, 0, TRIPS + i)
                    if layer:
                        store(BULK_TRIPS + 2 * i + 1, 1, TRIPS + i)

            bulk = BULK_TRIPS * 4
            sync.wait_ge(s_added, 16 * TILES * 4 + START_DMA)
            for u in range(2):
                sync.wait_ge(bulk_stored[u], 16 * bulk + START_DMA)
            with sync.Fori(0, BULK_TRIPS) as i:
                for u in range(2):
                    sync.wait_ge(bulk_used[u], bulk + i + START)
                    for k, t in ((0, base3_c), (1, agg3_c)):
                        sync.dma_start(bin_[:, u, k * C * D:(k + 1) * C * D].rearrange("p (c d) -> p c d", d=D),
                                       t[:, bass.ds((2 * i + u) * C, C), :]).then_inc((bulk_in, bulk_in2)[k][u], 16)

        @block.gpsimd
        def _(pool):
            steps = [0]

            def step(ins):
                steps[0] += 1
                ins.then_inc(s_pool, 1)
                pool.wait_ge(s_pool, steps[0])

            step(pool.memset(wide2[:, :], 0.0))
            step(pool.memset(wide3[:, :], 0.0))
            step(pool.memset(hidden, 1.0))
            pool.memset(zeros[:, :], 0.0).then_inc(s_built, 1)
            pool.wait_ge(s_built, 1)
            pool.dma_start(table0[NODES:ROWS, :].rearrange("(p c) w -> p c w", p=P),
                           zeros[:, 0:W0].rearrange("p (a w) -> p a w", a=1).to_broadcast([P, DUMP // P, W0]))\
                .then_inc(s_added, 16)
            step(pool.memset(ident[:, :], 0.0))
            step(pool.affine_select(out=ident[:, :], in_=ident[:, :], compare_op=ALU.not_equal, fill=1.0,
                                    base=0, pattern=[[-1, P]], channel_multiplier=1))
            step(pool.memset(earlier[:, :], 1.0))
            step(pool.affine_select(out=earlier[:, :], in_=earlier[:, :], compare_op=ALU.is_gt, fill=0.0,
                                    base=DUMP, pattern=[[-1, DUMP + P]], channel_multiplier=1))
            iota = seen_tmp[:, 0:TYPES].bitcast(i32)
            step(pool.iota(iota, pattern=[[1, TYPES]], base=0, channel_multiplier=0))
            step(pool.tensor_copy(type_iota[:, :], iota))
            iota = seen_tmp[:, TYPES:TYPES + TILES].bitcast(i32)
            step(pool.iota(iota.rearrange("p (g j) -> p g j", j=GROUP), pattern=[[0, TILES // GROUP], [P, GROUP]],
                           base=NODES, channel_multiplier=1))
            pool.tensor_copy(dump_row[:, :], iota).then_inc(s_iota, 1)

            pool.wait_ge(s_const, 16 * 18)
            for layer in range(4):
                if layer:
                    pool.wait_ge(s_added, 16 * TILES * layer + START_DMA)
                if layer != 1:
                    for u in range(2):
                        pool.wait_ge(bulk_stored[u], 16 * BULK_TRIPS * max(layer, 1) + START_DMA)
                table = (table0, table0, table1, table2)[layer]
                width = (W0, W0, W1, W2)[layer]
                key = dst_i if TO_SRC[layer] else src_i
                with pool.Fori(0, TRIPS) as i:
                    for u in range(2):
                        pool.wait_ge(rows_used[u], TRIPS * layer + i + START)
                        pool.tensor_copy(row_index[:, u, :], key[:, bass.ds((2 * i + u) * BATCH, BATCH)])\
                            .then_inc(index_in[u], 1)
                        pool.wait_ge(index_in[u], TRIPS * layer + i + 1)
                        apart(pool)
                        for k in range(BATCH):
                            pool.indirect_dma_start(
                                out=rows[:, u, k * width:(k + 1) * width], out_offset=None, in_=table,
                                in_offset=bass.IndirectOffsetOnAxis(ap=row_index[:, u, k:k + 1], axis=0),
                            ).then_inc(rows_in[u], 16)
                for u in range(2):
                    pool.wait_ge(rows_in[u], 16 * BATCH * TRIPS * (layer + 1))
                if layer:
                    pool.wait_ge(s_zero[layer], 16 * (CHUNKS + 1))
                to = (table0, table1, table2, agg3)[layer]
                first = (0, AGG, AGG, 0)[layer]
                width = (D + 1, D + 1, D, D)[layer]
                with pool.Fori(0, TRIPS) as i:
                    for v in range(GROUPS):
                        g = GROUPS * TRIPS * layer + GROUPS * i + v
                        pool.wait_ge(s_staged, g + 1 + START)
                        pool.wait_ge(s_added, 16 * GROUP * g + START_DMA)
                        apart(pool)
                        for k in range(GROUP):
                            pool.indirect_dma_start(
                                out=to, out_offset=bass.IndirectOffsetOnAxis(ap=to_index[:, v % 2, k:k + 1], axis=0),
                                in_=to_add[:, v % 2, k * width:(k + 1) * width], in_offset=None,
                                element_offset=first, compute_op=ALU.add,
                            ).then_inc(s_added, 16)

        @block.scalar
        def _(act):
            with act.Fori(0, BULK_TRIPS) as i:
                for u in range(2):
                    act.wait_ge(bulk_out[u], i + 1)
                    act.dma_start(table0_c[:, bass.ds((2 * i + u) * C, C), :],
                                  bout[:, u, :].rearrange("p (c w) -> p c w", w=W0)).then_inc(bulk_stored[u], 16)
            act.wait_ge(s_adapt, 1)
            act.activation(adapted[:, :], ps_gate[0][0:TYPES, 0:EMB], ACT.Copy).then_inc(s_adapted, 1)
            act.wait_ge(s_const, 16 * 18)
            with act.Fori(0, TILES // HALF) as i:
                act.wait_ge(s_hpre, i + 1 + START)
                act.wait_ge(s_gpre, i + START)
                act.activation(hidden[0:D, :].rearrange("p (b n) -> p b n", b=2),
                               ps_turn[0:D, :].rearrange("p (b n) -> p b n", b=2)[:, :, 0:HALF * P // 2],
                               ACT.Silu, bias=b1_sb[:, :]).then_inc(s_hid, 1)
                act.wait_ge(s_gpre, i + 1 + START)
                act.activation(gate[:, bass.ds(i * HALF, HALF), :],
                               ps_gate[0][:, 0:HALF * D].rearrange("p (t d) -> p t d", d=D), ACT.Copy).then_inc(s_gate, 1)
            act.wait_ge(s_ready, 1)
            act.activation(cw[:, :], cw[:, :], ACT.Sin, bias=half_pi[:, :], scale=-math.pi / 12).then_inc(s_ready, 1)
            act.wait_ge(s_ready, 2)
            act.activation(cw[:, :], cw[:, :], ACT.Square).then_inc(s_ready, 1)

            def group(layer, i, v):
                g = GROUPS * TRIPS * layer + GROUPS * i + v
                width = (D + 1, D + 1, D, D)[layer]
                to = src_to if TO_SRC[layer] else dst_to
                act.wait_ge(s_summed, g + 1 + START)
                act.wait_ge(s_added, (16 * GROUP * (g - 1 if v else g)) + START_DMA)
                act.activation(to_index[:, v % 2, :], to[:, bass.ds((GROUPS * i + v) * GROUP, GROUP)], ACT.Copy)
                act.activation(to_add[:, v % 2, 0:GROUP * width], ps_sum[v % 2][:, 0:GROUP * width], ACT.Copy)\
                    .then_inc(s_staged, 1)

            def square(centred, squared, n, dev, sq):
                act.wait_ge(centred, n + 1)
                act.activation(sq, dev, ACT.Square).then_inc(squared, 1)

            def root(ready, done, n, var, std):
                act.wait_ge(ready, n + 1)
                act.activation(std, var, ACT.Sqrt, bias=eps[:, :], scale=1.0 / D).then_inc(done, 1)

            def turn_copy(n):
                act.wait_ge(s_turned, n + 1 + START)
                act.activation(turned[0:2 * D, :], ps_turn[0:2 * D, 0:PAIRS * P], ACT.Copy).then_inc(s_turnc, 1)

            def edge(layer, i, u, part):
                b = 2 * i + u
                ln = {1: 0, 2: 14, 3: 42}.get(layer, 0)
                per = 2 if layer == 2 else 1
                n = ln + b * per
                mm = {2: 0, 3: 14}.get(layer, 0)
                if part == "centre":
                    square(e_dev, e_sqd, n, edev[:, :, :], esq[:, :, :])
                elif part == "var":
                    root(e_var, e_std, n, evar[:, :], estd[:, :])
                    if layer == 3:
                        act.wait_ge(s_deg, b + 1)
                        act.activation(efac[:, :], efac[:, :], ACT.Sqrt, bias=zero1[:, :]).then_inc(s_degroot, 1)
                elif part == "norm" and layer == 2:
                    square(e_dev, e_sqd, n + 1, edev[:, :, :], esq[:, :, :])
                elif part == "var2":
                    root(e_var, e_std, n + 1, evar[:, :], estd[:, :])
                elif part in ("onehot0", "onehot1"):
                    h = 2 * b + int(part[-1])
                    for k in range(2):
                        act.wait_ge(s_hott, 2 * h + k + 1 + START)
                        act.wait_ge(s_look, 2 * h + k + START)
                        act.activation(turned[0:TYPES, :], ps_turn[0:TYPES, 0:HALF * P], ACT.Copy).then_inc(s_hotc, 1)
                    act.wait_ge(s_look, 2 * h + 2 + START)
                    act.activation(ej[:, :, :], ps_prod[:, 512:512 + HALF * EMB].rearrange("p (t d) -> p t d", d=EMB),
                                   ACT.Copy).then_inc(s_ej, 1)
                elif part == "message" and layer > 1:
                    m = (b if layer == 2 else 14 + 3 * b)
                    turn_copy(m)
                    act.wait_ge(s_prod, m + 1)
                    act.activation(msg[:, bass.ds(b * BATCH, BATCH), 0:D].rearrange("p (q k) d -> p q k d", k=2),
                                   ps_prod[:, 0:PAIRS * P].rearrange("p (q n) -> p q n", n=P)[:, :, 0:2 * D]
                                   .rearrange("p q (k d) -> p q k d", k=2), ACT.Copy).then_inc(s_produsd, 1)

            def bulk(layer, q, part, m):
                n = {1: 0, 2: 28, 3: 84, 4: 112}[layer] + q * (2 if layer == 2 else 1)
                if part == "centre":
                    square(b_dev, b_sqd, n, bdev[:, :, :], bsq[:, :, :])
                elif part == "var":
                    root(b_var, b_std, n, bvar[:, :], bstd[:, :])
                elif part == "norm" and layer == 2:
                    square(b_dev, b_sqd, n + 1, bdev[:, :, :], bsq[:, :, :])
                elif part == "var2":
                    root(b_var, b_std, n + 1, bvar[:, :], bstd[:, :])
                elif part in ("mm0", "mm1"):
                    turn_copy(m)

            for layer in range(4):
                with act.Fori(0, TRIPS) as i:
                    for kind, u, part in gather_order(layer):
                        if kind == "edge":
                            edge(layer, i, u, part)
                        else:
                            m = 14 + 3 * (2 * i + u) + 1 + (part == "mm1")
                            bulk(layer, 2 * i + u, part, m)
                with act.Fori(0, TRIPS) as i:
                    for kind, k, part in scatter_order(layer):
                        if kind == "group":
                            group(layer, i, k)
                        else:
                            m = 14 + 3 * 14 + 2 * (2 * i + k) + (part == "mm1")
                            bulk(layer, BULK_TRIPS + 2 * i + k, part, m)
            with act.Fori(0, BULK_TRIPS) as i:
                for u in range(2):
                    bulk(4, 2 * i + u, "centre", 0)
                    bulk(4, 2 * i + u, "var", 0)
                    act.wait_ge(bulk_out[u], BULK_TRIPS * 4 + i + 1)
                    act.dma_start(out_c[:, bass.ds((2 * i + u) * C, C), :],
                                  bout[:, u, 0:C * D].rearrange("p (c d) -> p c d", d=D)).then_inc(bulk_stored[u], 16)
            for u in range(2):
                act.wait_ge(bulk_stored[u], 16 * BULK_TRIPS * 5 + START_DMA)

        @block.tensor
        def _(pe):
            pe.wait_ge(s_const, 16 * 18)
            pe.wait_ge(s_iota, 1)
            pe.matmul(ps_gate[0][0:TYPES, 0:EMB], lhsT=embt_sb[:, :], rhs=adapt_sb[:, :], start=True, stop=True)\
                .then_inc(s_adapt, 1)
            pe.wait_ge(s_adapted, 1)
            with pe.Fori(0, TILES // HALF // 2) as i:
                for u in range(2):
                    n = 2 * i + u
                    pe.wait_ge(attr_in[u], 16 * i + 16)
                    pe.wait_ge(s_hid, n + START)
                    apart(pe)
                    for k in range(2):
                        last = pe.matmul(ps_turn[0:D, k * 512:k * 512 + HALF * P // 2], lhsT=w1_sb[:, :],
                                         rhs=attr_sb[u][:, k * HALF * P // 2:(k + 1) * HALF * P // 2], start=True, stop=True)
                    last.then_inc(s_hpre, 1)
                    pe.wait_ge(s_hid, n + 1 + START)
                    pe.wait_ge(s_gate, n + START)
                    for k in range(HALF):
                        last = pe.matmul(ps_gate[0][:, k * D:(k + 1) * D], lhsT=hidden[0:D + 1, k * P:(k + 1) * P],
                                         rhs=w2_sb[:, :], start=True, stop=True)
                    last.then_inc(s_gpre, 1)

            def group(layer, i, v):
                g = GROUPS * TRIPS * layer + GROUPS * i + v
                width = (D + 1, D + 1, D, D)[layer]
                pe.wait_ge(s_same, g + 1 + START)
                pe.wait_ge(s_staged, (g - 1 if v else g) + START)
                for to in range(GROUP):
                    for of in range(GROUP):
                        last = pe.matmul(ps_sum[v % 2][:, to * width:(to + 1) * width],
                                         lhsT=same[:, v % 2, of, to * P:(to + 1) * P],
                                         rhs=msg[:, bass.ds((GROUPS * i + v) * GROUP + of, 1), 0:width]
                                         .rearrange("p a w -> p (a w)"), start=(of == 0), stop=(of == GROUP - 1))
                last.then_inc(s_summed, 1)

            def turn_multiply(n, of, wide):
                pe.wait_ge(s_mmin, n + 1)
                for q in range(PAIRS):
                    last = pe.transpose(ps_turn[0:2 * D, q * P:(q + 1) * P], of[:, q * 2 * D:(q + 1) * 2 * D], ident[:, :])
                last.then_inc(s_turned, 1)
                pe.wait_ge(s_turnc, n + 1)
                pe.wait_ge(s_produsd, n + START)
                for q in range(PAIRS):
                    last = pe.matmul(ps_prod[:, q * P:q * P + 2 * D], lhsT=turned[0:2 * D, q * P:(q + 1) * P],
                                     rhs=wide[:, :], start=True, stop=True)
                last.then_inc(s_prod, 1)

            edev_f = edev[:, :, :].rearrange("p t d -> p (t d)")
            bdev_f = bdev[:, :, :].rearrange("p t d -> p (t d)")

            def bulk(part, m):
                if part in ("mm0", "mm1"):
                    h = int(part[-1])
                    turn_multiply(m, bdev_f[:, h * BATCH * D:(h + 1) * BATCH * D], wide3)

            for layer in range(4):
                if layer:
                    with pe.Fori(0, TRIPS) as i:
                        for kind, u, part in gather_order(layer):
                            b = 2 * i + u
                            if kind == "bulk":
                                if layer == 3:
                                    bulk(part, 14 + 3 * b + 1 + (part == "mm1"))
                            elif part in ("onehot0", "onehot1"):
                                h = 2 * b + int(part[-1])
                                for k in range(2):
                                    pe.wait_ge(s_hot, 2 * h + k + 1)
                                    pe.wait_ge(s_hotc, 2 * h + k + START)
                                    for t in range(HALF):
                                        last = pe.transpose(ps_turn[0:TYPES, t * P:(t + 1) * P], onehot[:, k, t, :], ident[:, :])
                                    last.then_inc(s_hott, 1)
                                    pe.wait_ge(s_hotc, 2 * h + k + 1 + START)
                                    if k == 0:
                                        pe.wait_ge(s_lookused, h + START)
                                    for t in range(HALF):
                                        last = pe.matmul(ps_prod[:, k * 512 + t * EMB:k * 512 + (t + 1) * EMB],
                                                         lhsT=turned[0:TYPES, t * P:(t + 1) * P],
                                                         rhs=(emb_sb, adapted)[k][:, :], start=True, stop=True)
                                    last.then_inc(s_look, 1)
                            elif part == "message" and layer > 1:
                                turn_multiply(b if layer == 2 else 14 + 3 * b, edev_f, (wide2, wide3)[layer - 2])
                with pe.Fori(0, TRIPS) as i:
                    for kind, k, part in scatter_order(layer):
                        if kind == "group":
                            group(layer, i, k)
                        elif layer == 3:
                            bulk(part, 14 + 3 * 14 + 2 * (2 * i + k) + (part == "mm1"))

        @block.vector
        def _(dve):
            class Steps:
                base, k, i, per = 0, 0, None, 0

                def __call__(self, ins):
                    ins.then_inc(s_step, 1)
                    self.k += 1
                    done = self.base + self.k
                    dve.wait_ge(s_step, done if self.i is None else self.i * self.per + done)

            step = Steps()

            @contextmanager
            def loop(trips, per):
                with dve.Fori(0, trips) as i:
                    step.base, step.k, step.i, step.per = step.base + step.k, 0, i, per
                    yield i
                    assert step.k == per, step.k
                step.base, step.k, step.i = step.base + trips * per, 0, None

            def over(stat, k):
                return stat.rearrange("p (t a) -> p t a", a=1).to_broadcast([P, k, D])

            def along(vec, k):
                return vec[:, :].rearrange("p (a d) -> p a d", a=1).to_broadcast([P, k, D])

            dve.memset(eps[:, :], EPS)
            dve.memset(half_pi[:, :], math.pi / 2)
            step(dve.memset(zero1[:, :], 0.0))
            step(dve.memset(bout[:, :, :], 0.0))
            for u in range(2):
                dve.wait_ge(bulk_stored[u], START_DMA)
            mult_c = mult_in.rearrange("p (c a) -> p c a", a=1)
            type_c = type_in.rearrange("p (c a) -> p c a", a=1)
            with dve.Fori(0, BULK_TRIPS) as i:
                for u in range(2):
                    o = bout[:, u, :].rearrange("p (c w) -> p c w", w=W0)
                    at = bass.ds((2 * i + u) * C, C)
                    dve.wait_ge(bulk_in[u], 16 * i + 16)
                    dve.wait_ge(bulk_stored[u], 16 * i + START_DMA)
                    dve.tensor_copy(o[:, :, 0:D], bin_[:, u, 0:C * D].rearrange("p (c d) -> p c d", d=D))\
                        .then_inc(bulk_used[u], 1)
                    dve.tensor_copy(o[:, :, MULT:MULT + 1], mult_c[:, at, :])
                    dve.tensor_copy(o[:, :, TYPE:TYPE + 1], type_c[:, at, :]).then_inc(bulk_out[u], 1)
            dve.wait_ge(s_const, 16 * 18)
            dve.wait_ge(s_iota, 1)
            step(dve.tensor_copy(src_f[:, :], src_i[:, :]))
            step(dve.tensor_copy(dst_f[:, :], dst_i[:, :]))
            dve.tensor_scalar(cw[:, :], ew[:, :], 6.0, None, ALU.min).then_inc(s_ready, 1)
            step(dve.memset(msg[:, :, D:D + 1], 1.0))

            same_key = (dst_f, src_f, src_f, dst_f)

            def counts(i, v):
                g = GROUPS * i + v
                per = 4 if v % 2 == 0 else 3
                dve.wait_ge(key_in[v % 2], i * (per * 32) + (v // 2 + 1) * 32)
                for k, (key, seen) in enumerate(((dst_f, dst_seen), (src_f, src_seen))):
                    for j in range(GROUP):
                        at = bass.ds(g * GROUP + j, 1)
                        last = dve.scalar_tensor_tensor(
                            seen_tmp[:, 0:(j + 1) * P], keyrow[:, v % 2, k, 0:(j + 1) * P], key[:, at],
                            earlier[:, DUMP - j * P:DUMP + P], ALU.is_equal, ALU.mult, accum_out=seen[:, at])
                        if k == 0 or j < GROUP - 1:
                            step(last)
                last.then_inc(s_counted, 1)
                dve.wait_ge(s_counted, g + 1 + START)

            def group(layer, i, v):
                g = GROUPS * TRIPS * layer + GROUPS * i + v
                per = 4 if v % 2 == 0 else 3
                before = TRIPS * per * (32 + 16 * layer)
                dve.wait_ge(key_in[v % 2], before + i * (per * 16) + (v // 2 + 1) * 16)
                dve.wait_ge(s_summed, (g - 1 if v else g) + START)
                for j in range(GROUP):
                    last = dve.tensor_scalar(same[:, v % 2, j, :], keyrow[:, v % 2, TO_SRC[layer], :],
                                             same_key[layer][:, bass.ds((GROUPS * i + v) * GROUP + j, 1)], None, ALU.is_equal)
                last.then_inc(s_same, 1)

            def centre(of, total, dev, k, ready):
                step(dve.reduce_sum(total[:, :], of, AX.X))
                dve.scalar_tensor_tensor(dev, over(total[:, :], k), -1.0 / D, of, ALU.mult, ALU.add).then_inc(ready, 1)

            def variance(sq, squared, n, var, ready):
                dve.wait_ge(squared, n + 1)
                dve.reduce_sum(var[:, :], sq, AX.X).then_inc(ready, 1)

            def normed(to, dev, std, done, n, k, free=None):
                dve.wait_ge(done, n + 1)
                ins = dve.reciprocal(std[:, :], std[:, :])
                if free:
                    ins.then_inc(free[0], 1)
                    dve.wait_ge(*free)
                else:
                    step(ins)
                return dve.tensor_tensor(to, dev, over(std[:, :], k), ALU.mult)

            def residual(row, tmp, tmp1, k):
                step(dve.tensor_scalar(tmp1[:, :], row[:, :, TOT:TOT + 1].rearrange("p t a -> p (t a)"), 1e-8, None, ALU.max))
                step(dve.reciprocal(tmp1[:, :], tmp1[:, :]))
                step(dve.tensor_tensor(tmp, row[:, :, AGG:AGG + D], over(tmp1[:, :], k), ALU.mult))
                step(dve.tensor_tensor(tmp, tmp, row[:, :, 0:D], ALU.add))

            def inner_out(row, dev, k):
                step(dve.tensor_tensor(dev, dev, along(gamma_b, k), ALU.mult))
                step(dve.tensor_tensor(dev, dev, along(beta_b, k), ALU.add))
                step(dve.tensor_tensor(dev, dev, row[:, :, 0:D], ALU.add))

            ED, ESQ, BD, BSQ = edev[:, :, :], esq[:, :, :], bdev[:, :, :], bsq[:, :, :]

            def edge(layer, i, u, part):
                b = 2 * i + u
                width = (W0, W0, W1, W2)[layer]
                row = rows[:, u, 0:BATCH * width].rearrange("p (t w) -> p t w", w=width)
                tiles = bass.ds(b * BATCH, BATCH)
                n = {0: 0, 1: 0, 2: 14, 3: 42}[layer] + b * (2 if layer == 2 else 1)
                if part == EDGE_PARTS[layer][0]:
                    dve.wait_ge(rows_in[u], 16 * BATCH * (TRIPS * layer + i + 1))
                if layer == 0:
                    dve.tensor_tensor(msg[:, tiles, 0:D], row[:, :, 0:D], over(ew[:, tiles], BATCH), ALU.mult)
                    dve.tensor_copy(src_type[:, tiles], row[:, :, TYPE:TYPE + 1].rearrange("p t a -> p (t a)"))\
                        .then_inc(rows_used[u], 1)
                elif part == "centre":
                    if layer > 1:
                        dve.wait_ge(s_turned, (b if layer == 2 else 14 + 3 * b) + START)
                    if layer == 1:
                        centre(row[:, :, 0:D], esum, ED, BATCH, e_dev)
                    elif layer == 2:
                        residual(row, ESQ, efac, BATCH)
                        centre(ESQ, esum, ED, BATCH, e_dev)
                    else:
                        step(dve.tensor_tensor(ESQ, row[:, :, 0:D], row[:, :, AGG:AGG + D], ALU.add))
                        centre(ESQ, esum, ED, BATCH, e_dev)
                elif part in ("onehot0", "onehot1"):
                    h = int(part[-1])
                    half = row[:, h * HALF:(h + 1) * HALF, TYPE:TYPE + 1]
                    iota = type_iota[:, :].rearrange("p (a n) -> p a n", a=1).to_broadcast([P, HALF, TYPES])
                    at = bass.ds(b * BATCH + h * HALF, HALF)
                    dve.wait_ge(s_hott, 4 * b + 2 * h + START)
                    dve.tensor_tensor(onehot[:, 0, :, :], iota,
                                      src_type[:, at].rearrange("p (t a) -> p t a", a=1).to_broadcast([P, HALF, TYPES]),
                                      ALU.is_equal).then_inc(s_hot, 1)
                    dve.tensor_tensor(onehot[:, 1, :, :], iota, half.to_broadcast([P, HALF, TYPES]),
                                      ALU.is_equal).then_inc(s_hot, 1)
                elif part in ("logit0", "logit1"):
                    h = int(part[-1])
                    dve.wait_ge(s_ej, 2 * b + h + 1)
                    dve.tensor_tensor(eij[:, :, :], ps_prod[:, 0:HALF * EMB].rearrange("p (t d) -> p t d", d=EMB),
                                      ej[:, :, :], ALU.mult).then_inc(s_lookused, 1)
                    dve.wait_ge(s_lookused, 2 * b + h + 1 + START)
                    step(dve.reduce_sum(logit[:, h * HALF:(h + 1) * HALF], eij[:, :, :], AX.X))
                elif part == "var":
                    variance(ESQ, e_sqd, n, evar, e_var)
                    if layer == 3:
                        step(dve.tensor_scalar(efac2[:, :], dst_deg[:, tiles], 1.0, None, ALU.add))
                        dve.scalar_tensor_tensor(efac[:, :], row[:, :, DEG:DEG + 1].rearrange("p t a -> p (t a)"), 1.0,
                                                 efac2[:, :], ALU.add, ALU.mult).then_inc(s_deg, 1)
                elif part == "norm":
                    step(normed(ED, ED, estd, e_std, n, BATCH))
                    if layer == 2:
                        inner_out(row, ED, BATCH)
                        dve.reduce_sum(esum[:, :], ED, AX.X).then_inc(rows_used[u], 1)
                        dve.wait_ge(rows_used[u], TRIPS * layer + i + 1 + START)
                        dve.scalar_tensor_tensor(ED, over(esum[:, :], BATCH), -1.0 / D, ED, ALU.mult, ALU.add)\
                            .then_inc(e_dev, 1)
                elif part == "var2":
                    variance(ESQ, e_sqd, n + 1, evar, e_var)
                elif layer == 1:
                    mult = row[:, :, MULT:MULT + 1].rearrange("p t a -> p (t a)")
                    dve.tensor_copy(dst_deg[:, tiles], row[:, :, DEG:DEG + 1].rearrange("p t a -> p (t a)"))
                    dve.tensor_copy(msg[:, tiles, D:D + 1], row[:, :, MULT:MULT + 1])
                    step(dve.tensor_tensor(efac[:, :], cw[:, tiles], mult, ALU.mult))
                    step(dve.tensor_tensor(msg[:, tiles, 0:D], gate[:, tiles, :], over(logit[:, :], BATCH), ALU.add))
                    step(dve.tensor_tensor(msg[:, tiles, 0:D], msg[:, tiles, 0:D], over(efac[:, :], BATCH), ALU.mult))
                    dve.tensor_tensor(msg[:, tiles, 0:D], msg[:, tiles, 0:D], ED, ALU.mult).then_inc(rows_used[u], 1)
                elif layer == 2:
                    step(normed(ED, ED, estd, e_std, n + 1, BATCH))
                    dve.tensor_tensor(ED, ED, over(ew[:, tiles], BATCH), ALU.mult).then_inc(s_mmin, 1)
                else:
                    dve.wait_ge(s_degroot, b + 1)
                    dve.reciprocal(efac[:, :], efac[:, :]).then_inc(rows_used[u], 1)
                    dve.wait_ge(rows_used[u], TRIPS * layer + i + 1 + START)
                    dve.wait_ge(e_std, n + 1)
                    step(dve.reciprocal(estd[:, :], estd[:, :]))
                    step(dve.tensor_tensor(efac[:, :], efac[:, :], estd[:, :], ALU.mult))
                    dve.tensor_tensor(ED, ED, over(efac[:, :], BATCH), ALU.mult).then_inc(s_mmin, 1)

            def bulk(layer, q, u, ii, part, m):
                width = (0, W0, W1, W2)[layer]
                row = bin_[:, u, 0:C * width].rearrange("p (c w) -> p c w", w=width)
                wo = (0, D + 1, D + 1, D)[layer]
                o = bout[:, u, 0:C * wo].rearrange("p (c w) -> p c w", w=wo)
                n = {1: 0, 2: 28, 3: 84}[layer] + q * (2 if layer == 2 else 1)
                done = BULK_TRIPS * layer + ii
                if part == "centre":
                    dve.wait_ge(bulk_in[u], 16 * (done + 1))
                    dve.wait_ge(bulk_stored[u], 16 * done + START_DMA)
                    if layer < 3:
                        dve.tensor_copy(o[:, :, D:D + 1], row[:, :, DEG:DEG + 1])
                    if layer == 1:
                        centre(row[:, :, 0:D], bsum, BD, C, b_dev)
                    elif layer == 2:
                        residual(row, BSQ, bfac, C)
                        centre(BSQ, bsum, BD, C, b_dev)
                    else:
                        dve.wait_ge(bulk_out[1 - u], done + u)
                        step(dve.tensor_tensor(BSQ, row[:, :, 0:D], row[:, :, AGG:AGG + D], ALU.add))
                        centre(BSQ, bsum, BD, C, b_dev)
                elif part == "var":
                    variance(BSQ, b_sqd, n, bvar, b_var)
                    if layer == 3:
                        step(dve.tensor_scalar(bfac[:, :], row[:, :, DEG:DEG + 1].rearrange("p t a -> p (t a)"), 1.0, None, ALU.add))
                        dve.reciprocal(bfac[:, :], bfac[:, :]).then_inc(bulk_used[u], 1)
                        dve.wait_ge(bulk_used[u], done + 1 + START)
                elif part == "norm":
                    if layer == 1:
                        normed(o[:, :, 0:D], BD, bstd, b_std, n, C, (bulk_used[u], done + 1 + START)).then_inc(bulk_out[u], 1)
                    elif layer == 2:
                        step(normed(BD, BD, bstd, b_std, n, C))
                        inner_out(row, BD, C)
                        dve.reduce_sum(bsum[:, :], BD, AX.X).then_inc(bulk_used[u], 1)
                        dve.wait_ge(bulk_used[u], done + 1 + START)
                        dve.scalar_tensor_tensor(BD, over(bsum[:, :], C), -1.0 / D, BD, ALU.mult, ALU.add).then_inc(b_dev, 1)
                    else:
                        normed(BD, BD, bstd, b_std, n, C).then_inc(s_mmin, 1)
                        dve.wait_ge(s_mmin, m + 1)
                        dve.tensor_tensor(BSQ, BD, along(bias3_b, C), ALU.add).then_inc(s_mmin, 1)
                elif part == "var2":
                    variance(BSQ, b_sqd, n + 1, bvar, b_var)
                elif part == "norm2":
                    step(normed(BD, BD, bstd, b_std, n + 1, C))
                    dve.tensor_tensor(o[:, :, 0:D], BD, along(bias2_b, C), ALU.add).then_inc(bulk_out[u], 1)
                else:
                    h = int(part[-1])
                    half = o[:, h * BATCH:(h + 1) * BATCH, :]
                    dve.wait_ge(s_prod, m + 1)
                    prod = ps_prod[:, 0:PAIRS * P].rearrange("p (q n) -> p q n", n=P)[:, :, 0:2 * D]
                    fac = bfac[:, h * BATCH:(h + 1) * BATCH].rearrange("p (q k a) -> p q k a", k=2, a=1)
                    dve.tensor_tensor(half.rearrange("p (q k) d -> p q k d", k=2), prod.rearrange("p q (k d) -> p q k d", k=2),
                                      fac.to_broadcast([P, PAIRS, 2, D]), ALU.mult).then_inc(s_produsd, 1)
                    dve.wait_ge(s_produsd, m + 1 + START)
                    last = dve.tensor_tensor(half, half, BSQ[:, h * BATCH:(h + 1) * BATCH, :], ALU.add)
                    if h:
                        last.then_inc(bulk_out[u], 1)

            for layer in range(4):
                if layer == 1:
                    dve.wait_ge(s_gate, TILES // HALF + START)
                    dve.wait_ge(s_ready, 3)
                with loop(TRIPS, PER_GATHER[layer]) as i:
                    if layer == 0:
                        for v in range(GROUPS):
                            counts(i, v)
                            if v in (2, 5):
                                edge(0, i, v // 3, "message")
                    else:
                        for kind, u, part in gather_order(layer):
                            if kind == "edge":
                                edge(layer, i, u, part)
                            else:
                                m = 14 + 3 * (2 * i + u) + 1 + (part == "mm1")
                                bulk(layer, 2 * i + u, u, i, part, m)
                if layer == 0:
                    dve.wait_ge(s_counted, GROUPS * TRIPS + START)
                    for key, seen, to in ((dst_f, dst_seen, dst_to), (src_f, src_seen, src_to)):
                        tmp = seen_tmp[:, 0:TILES]
                        step(dve.tensor_scalar(seen[:, :], seen[:, :], 1.0, None, ALU.min))
                        step(dve.tensor_tensor(tmp, dump_row[:, :], key[:, :], ALU.subtract))
                        step(dve.tensor_tensor(tmp, tmp, seen[:, :], ALU.mult))
                        step(dve.tensor_tensor(to[:, :], key[:, :], tmp, ALU.add))
                with loop(TRIPS, PER_SCATTER[layer]) as i:
                    for kind, k, part in scatter_order(layer):
                        if kind == "group":
                            group(layer, i, k)
                        else:
                            m = 14 + 3 * 14 + 2 * (2 * i + k) + (part == "mm1")
                            bulk(layer, BULK_TRIPS + 2 * i + k, k, TRIPS + i, part, m)
            with loop(BULK_TRIPS, PER_LAST) as i:
                for u in range(2):
                    n = 112 + 2 * i + u
                    base = bin_[:, u, 0:C * D].rearrange("p (c d) -> p c d", d=D)
                    sums = bin_[:, u, C * D:2 * C * D].rearrange("p (c d) -> p c d", d=D)
                    o = bout[:, u, 0:C * D].rearrange("p (c d) -> p c d", d=D)
                    dve.wait_ge(bulk_in[u], 16 * (BULK_TRIPS * 4 + i + 1))
                    dve.wait_ge(bulk_in2[u], 16 * (i + 1))
                    dve.tensor_tensor(BSQ, base, sums, ALU.add).then_inc(bulk_used[u], 1)
                    dve.wait_ge(bulk_used[u], BULK_TRIPS * 4 + i + 1 + START)
                    centre(BSQ, bsum, BD, C, b_dev)
                    variance(BSQ, b_sqd, n, bvar, b_var)
                    dve.wait_ge(bulk_stored[u], 16 * (BULK_TRIPS * 4 + i) + START_DMA)
                    normed(o, BD, bstd, b_std, n, C).then_inc(bulk_out[u], 1)


_PADDED = EDGES - E


def kernel(x, src, dst, edge_attr_40, edge_weight, node_type_119, node_vec, L1_gnn_W1, L1_gnn_b1, L1_gnn_W2,
           L1_gnn_b2, L1_gnn_emb, L1_gnn_adaptW, L1_gnn_gamma, L1_gnn_beta, L2_gnn_weight, L2_gnn_bias,
           L3_gnn_W, L3_gnn_b):
    import numpy as np
    import concourse.bacc as bacc
    from concourse.bass_utils import run_bass_kernel_spmd

    def padded(a, n):
        out = np.zeros((n, *a.shape[1:]), a.dtype)
        out[:len(a)] = a
        return out

    def edge_keys(a):
        return np.concatenate([a, np.arange(N, N + _PADDED, dtype=a.dtype)])

    def tiles(a):
        return np.ascontiguousarray(a.reshape(TILES, P).T)

    t = np.ascontiguousarray
    src, dst = edge_keys(np.asarray(src)), edge_keys(np.asarray(dst))
    arrays = {
        "x": padded(np.asarray(x), NODES), "node_mult": padded(np.asarray(node_vec), NODES),
        "node_type": padded(np.asarray(node_type_119), NODES),
        "src_rows": src.reshape(1, EDGES), "dst_rows": dst.reshape(1, EDGES),
        "src_tiles": tiles(src), "dst_tiles": tiles(dst),
        "attr_t": t(padded(np.asarray(edge_attr_40), EDGES).T), "weight_tiles": tiles(padded(np.asarray(edge_weight), EDGES)),
        "w1_t": t(np.asarray(L1_gnn_W1).T), "b1": np.asarray(L1_gnn_b1), "w2_t": t(np.asarray(L1_gnn_W2).T),
        "b2": np.asarray(L1_gnn_b2), "emb": np.asarray(L1_gnn_emb), "emb_t": t(np.asarray(L1_gnn_emb).T),
        "adapt_t": t(np.asarray(L1_gnn_adaptW).T), "gamma": np.asarray(L1_gnn_gamma), "beta": np.asarray(L1_gnn_beta),
        "weight2": np.asarray(L2_gnn_weight), "bias2": np.asarray(L2_gnn_bias),
        "weight3": np.asarray(L3_gnn_W), "bias3": np.asarray(L3_gnn_b),
    }
    nc = bacc.Bacc("TRN2", target_bir_lowering=False, num_devices=1)
    args = {n: nc.dram_tensor(n, a.shape, mybir.dt.from_np(a.dtype), kind="ExternalInput").ap() for n, a in arrays.items()}
    out = nc.dram_tensor("out", [NODES, D], mybir.dt.float32, kind="ExternalOutput").ap()
    graph_layers(nc, out=out, **args)
    r = run_bass_kernel_spmd(nc, [arrays], core_ids=[0])
    return r.results[0]["out"][:N]
```

```python
import math
from contextlib import ExitStack, contextmanager

import concourse.bass as bass
from concourse import mybir

P = 128
N, E, D = 100000, 25000, 48
R, TYPES, EMB = 40, 119, 32
BATCH = 14
GROUP = 4
PAIRS = BATCH // 2
TILES = 196
CHUNKS = 28
C = 28
HALF = 7
NODES = P * CHUNKS * C
EDGES = TILES * P
DUMP = GROUP * P
ROWS = NODES + DUMP
TRIPS = 7
BATCHES, GROUPS, BLOCKS = 2, TILES // GROUP // TRIPS, TILES // HALF // TRIPS
BULK_TRIPS = 2 * TRIPS
EPS = 1e-5
W = D + 1
DEG, MULT, TYPE, W0 = D, D + 1, D + 2, D + 4
AGG, TOT, W1 = D + 1, 2 * D + 1, 2 * D + 2
W2 = 2 * D + 1

assert TILES == TRIPS * BATCHES * BATCH == TRIPS * GROUPS * GROUP and EDGES >= E
assert NODES >= N + EDGES - E

START, START_DMA = 1, 16
TO_SRC = (0, 1, 1, 0)
PER_GATHER = (49, 14, 18, 10)
PER_SCATTER = (0, 2, 8, 4)
PER_LAST = 0
PER_FIRST = 2

EDGE_PARTS = (["message", "split"],
              ["hot", "var", "norm", "logit", "message", "split"],
              ["rescale", "var", "norm", "gamma", "var2", "scale", "weight", "split"],
              ["sum", "var", "scale", "weight", "split"])
BULK_PARTS = ([],
              ["square", "var", "norm"],
              ["rescale", "var", "norm", "gamma0", "gamma1", "var2", "norm2"],
              ["sum", "var", "norm", "mm0", "mm1"])
PRODUCTS = ("gamma", "weight", "gamma0", "gamma1", "mm0", "mm1")
EDGE_NORMS, BULK_NORMS, EDGE_INPUTS, BULK_INPUTS = (0, 0, 7, 21), (0, 0, 14, 42, 56), (0, 0, 0, 14), (0, 0, 0, 14)


def spread(streams):
    timed = [(a + (b - a) * (k + 0.5) / len(items), n, x)
             for n, (a, b, items) in enumerate(streams) for k, x in enumerate(items)]
    return [x for _, _, x in sorted(timed, key=lambda y: y[:2])]


def gather_order(layer):
    streams = [(0.4 * u, 0.4 * u + 0.6, [(kind, u, x) for x in parts[layer]])
               for u in range(2) for kind, parts in (("edge", EDGE_PARTS), ("bulk", BULK_PARTS))]
    if layer == 0:
        streams += [(0, 1, [("count", v, None) for v in range(GROUPS)]), (0, 1, [("gate", w, None) for w in range(BLOCKS)])]
    return spread([x for x in streams if x[2]])


def scatter_order(layer):
    streams = [(0, 1, [("group", v, None) for v in range(GROUPS)])]
    if layer == 0:
        streams += [(0.5 * u, 0.5 * u + 0.5, [("look", u, "hot"), ("look", u, "store")]) for u in range(2)]
    streams += [(0.4 * u, 0.4 * u + 0.6, [("bulk", u, x) for x in BULK_PARTS[layer]]) for u in range(2)]
    return spread([x for x in streams if x[2]])


ORDERS = [(gather_order(layer), scatter_order(layer)) for layer in range(4)]


def product_number(layer, phase, i, item):
    made = [[[x for x in order if x[2] in PRODUCTS] for order in both] for both in ORDERS]
    before = sum(TRIPS * len(made[a][b]) for a in range(4) for b in range(2) if (a, b) < (layer, phase))
    here = made[layer][phase]
    return before + len(here) * i + here.index(item)


def graph_layers(nc, x, node_mult, node_type, src_rows, dst_rows, src_tiles, dst_tiles, attr_t, weight_tiles,
                 w1_t, b1, w2_t, b2, emb, emb_t, adapt_t, gamma, beta, weight2, bias2, weight3, bias3, out):
    f32, i32, bf16 = mybir.dt.float32, mybir.dt.int32, mybir.dt.bfloat16
    ALU, ACT, AX = mybir.AluOpType, mybir.ActivationFunctionType, mybir.AxisListType

    def dram(name, shape):
        return nc.dram_tensor(name, shape, f32, kind="Internal").ap()

    table0, table1, table2 = dram("table0", [ROWS, W0]), dram("table1", [ROWS, W1]), dram("table2", [ROWS, W2])
    base3, agg3 = dram("base3", [NODES, D]), dram("agg3", [ROWS, D])
    gates, src_emb = dram("gates", [P, TILES * D]), dram("src_emb", [P, TILES * EMB])

    def by_chunk(t):
        return t[0:NODES, :].rearrange("(p c) w -> p c w", p=P)

    x_c, table0_c, table1_c, table2_c = by_chunk(x), by_chunk(table0), by_chunk(table1), by_chunk(table2)
    base3_c, agg3_c, out_c = by_chunk(base3), by_chunk(agg3), by_chunk(out)

    ctx = ExitStack()
    with ctx:
        def sb(name, shape, dt=f32):
            return ctx.enter_context(nc.sbuf_tensor(name, shape, dt))

        def sem(name):
            return ctx.enter_context(nc.semaphore(name))

        def pair(name):
            return [sem(f"{name}_{u}") for u in range(2)]

        ident = sb("ident", [P, P])
        ident_b = sb("ident_b", [P, P], bf16)
        earlier = sb("earlier", [P, DUMP + P])
        type_iota = sb("type_iota", [P, TYPES])
        dump_row = sb("dump_row", [P, TILES])
        zeros = sb("zeros", [P, W1])
        eps = sb("eps", [P, 1])
        half_pi = sb("half_pi", [P, 1])
        zero1 = sb("zero1", [P, 1])
        gamma_b = sb("gamma_b", [P, D])
        beta_b = sb("beta_b", [P, D])
        bias2_b = sb("bias2_b", [P, D])
        bias3_b = sb("bias3_b", [P, D])
        w1_sb = sb("w1_sb", [R, D])
        b1_sb = sb("b1_sb", [D, 1])
        w2_sb = sb("w2_sb", [D + 1, D])
        emb_sb = sb("emb_sb", [TYPES, EMB])
        embt_sb = sb("embt_sb", [EMB, TYPES])
        adapt_sb = sb("adapt_sb", [EMB, EMB])
        adapted = sb("adapted", [TYPES, EMB])
        emb_rest = sb("emb_rest", [TYPES, EMB])
        emb_parts = sb("emb_parts", [TYPES, 3, EMB], bf16)
        adapted_parts = sb("adapted_parts", [TYPES, 3, EMB], bf16)
        wide2 = sb("wide2", [2 * D, 2 * D])
        wide3 = sb("wide3", [2 * D, 2 * D])
        wide_gamma = sb("wide_gamma", [2 * D + 1, 2 * D])
        wide_mean = sb("wide_mean", [P, 2])
        src_i = sb("src_i", [P, TILES], i32)
        dst_i = sb("dst_i", [P, TILES], i32)
        src_f = sb("src_f", [P, TILES])
        dst_f = sb("dst_f", [P, TILES])
        ew = sb("ew", [P, TILES])
        cw = sb("cw", [P, TILES])
        src_seen = sb("src_seen", [P, TILES])
        dst_seen = sb("dst_seen", [P, TILES])
        src_to = sb("src_to", [P, TILES], i32)
        dst_to = sb("dst_to", [P, TILES], i32)
        src_type = sb("src_type", [P, TILES])
        dst_deg = sb("dst_deg", [P, TILES])
        parts = sb("parts", [P, TILES, 3, W], bf16)
        mult_in = sb("mult_in", [P, CHUNKS * C])
        type_in = sb("type_in", [P, CHUNKS * C], i32)
        rows = sb("rows", [P, 2, BATCH * W1])
        row_index = sb("row_index", [P, 2, BATCH], i32)
        edev = sb("edev", [P, 2, BATCH, D])
        esq = sb("esq", [P, 2, BATCH, D])
        emsg = sb("emsg", [P, 2, BATCH, W])
        erest = sb("erest", [P, 2, BATCH, W])
        evar = sb("evar", [P, 2, BATCH])
        estd = sb("estd", [P, 2, BATCH])
        efac = sb("efac", [P, 2, BATCH])
        efac2 = sb("efac2", [P, 2, BATCH])
        logit = sb("logit", [P, 2, BATCH])
        gate_in = sb("gate_in", [P, 2, BATCH, D])
        emb_in = sb("emb_in", [P, 2, BATCH, EMB])
        onehot = sb("onehot", [P, BATCH, TYPES], bf16)
        hot_turned = sb("hot_turned", [P, BATCH * P], bf16)
        looked = sb("looked", [P, BATCH, EMB])
        turned = sb("turned", [P, PAIRS * P])
        keyrow = sb("keyrow", [P, 2, 2, DUMP], i32)
        same = sb("same", [P, 2, GROUP, DUMP], bf16)
        to_add = sb("to_add", [P, 2, GROUP * W])
        to_index = sb("to_index", [P, 2, GROUP], i32)
        bin_ = sb("bin", [P, 2, C * W1])
        bout = sb("bout", [P, 2, C * W0])
        bdev = sb("bdev", [P, 2, C, D])
        bsq = sb("bsq", [P, 2, C, D])
        bvar = sb("bvar", [P, 2, C])
        bstd = sb("bstd", [P, 2, C])
        bfac = sb("bfac", [P, 2, C])
        attr_sb = [bsq[0:R, u, :, :].rearrange("p c d -> p (c d)")[:, 0:HALF * P] for u in range(2)]
        hidden = bdev[0:64, 0, :, :].rearrange("p c d -> p (c d)")[:, 0:HALF * P]
        gate_out = bdev[:, 1, 0:HALF, :]
        seen_tmp = edev[:, 0, :, :].rearrange("p b d -> p (b d)")

        ps = ctx.enter_context(nc.psum_tensor("ps", [P, 8, 512], f32))
        flat = ps[:, :, :].rearrange("p b n -> p (b n)")
        ps_turn, ps_prod = flat[:, 0:1024], flat[:, 1024:2048]
        ps_gate, ps_look = ps[:, 2, :], ps[:, 3, :]
        ps_sum = [ps[:, 4, :], ps[:, 5, :]]
        ps_hot = flat[:, 3072:4096].bitcast(bf16)

        def top_half(t):
            return t.bitcast(bf16).rearrange("p (n h) -> p n h", h=2)[:, :, 1:2].rearrange("p n h -> p (n h)")

        s_const = sem("const_loaded")
        s_built = sem("const_built")
        s_iota = sem("iota_made")
        s_pool = sem("pool_step")
        s_ready = sem("edge_arrays_ready")
        s_centred = sem("weights_centred")
        s_adapt = sem("adapted_product")
        s_adapted = sem("adapted_ready")
        bulk_in, bulk_in2 = pair("bulk_loaded"), pair("bulk_loaded_sum")
        bulk_used, bulk_out, bulk_stored = pair("bulk_used"), pair("bulk_ready"), pair("bulk_stored")
        attr_in = pair("attr_loaded")
        s_hpre, s_hid = sem("hidden_product"), sem("hidden_ready")
        s_gpre, s_gate, s_gstored = sem("gate_product"), sem("gate_ready"), sem("gate_stored")
        s_estored = sem("src_emb_stored")
        s_zero = [sem(f"sums_started_{k}") for k in range(4)]
        key_in, rows_in, rows_used, index_in = pair("keyrow_loaded"), pair("rows_gathered"), pair("rows_used"), pair("index_staged")
        side_in, side_used = pair("gate_and_emb_loaded"), pair("gate_and_emb_used")
        s_counted = sem("keys_counted")
        s_same, s_summed, s_staged, s_added = sem("same_ready"), sem("sum_product"), sem("sum_staged"), sem("group_added")
        e_dev, e_sqd, e_var, e_std = pair("edge_state"), pair("edge_squared"), pair("edge_variance"), pair("edge_deviation")
        b_dev, b_sqd, b_var, b_std = pair("bulk_state"), pair("bulk_squared"), pair("bulk_variance"), pair("bulk_deviation")
        s_deg, s_degroot = pair("degree_product"), pair("degree_root")
        s_msg, s_rest, s_parts = pair("message_ready"), pair("message_rest"), pair("message_parts")
        s_step = sem("vector_step")
        s_hot, s_hott, s_hotc = sem("onehot_ready"), sem("onehot_turned"), sem("onehot_turned_copied")
        s_look, s_looked = sem("types_looked_up"), sem("lookup_taken")
        e_input, b_input = pair("edge_product_input"), pair("bulk_product_input")
        s_turned, s_turnc = sem("input_turned"), sem("input_turned_copied")
        s_prod, s_taken = sem("product_ready"), sem("product_taken")

        block = ctx.enter_context(nc.Block())

        def apart(engine):
            engine.nop(nofuse=True)

        @block.sync
        def _(sync):
            n = [0]

            def const(to, of):
                sync.dma_start(to, of).then_inc(s_const, 16)
                n[0] += 1

            for started in (*bulk_used, *rows_used, *side_used, *s_parts, s_counted, s_hpre, s_same, s_staged, s_summed,
                            s_hid, s_gate, s_gpre, s_hott, s_hotc, s_look, s_looked, s_taken):
                sync.sem_inc(started, START)
            sync.dma_start(mult_in[:, :], node_mult.rearrange("(p c) -> p c", p=P)).then_inc(bulk_stored[0], 16)
            sync.dma_start(type_in[:, :], node_type.rearrange("(p c) -> p c", p=P)).then_inc(bulk_stored[1], 16)
            with sync.Fori(0, BULK_TRIPS) as i:
                for u in range(2):
                    sync.wait_ge(bulk_used[u], i + START)
                    sync.dma_start(bin_[:, u, 0:C * D].rearrange("p (c d) -> p c d", d=D),
                                   x_c[:, bass.ds((2 * i + u) * C, C), :]).then_inc(bulk_in[u], 16)
            sync.wait_ge(s_built, 1)
            const(src_i[:, :], src_tiles)
            const(dst_i[:, :], dst_tiles)
            const(ew[:, :], weight_tiles)
            for to, of in ((gamma_b, gamma), (beta_b, beta), (bias2_b, bias2), (bias3_b, bias3)):
                const(to[:, :], of.rearrange("(a d) -> a d", a=1).to_broadcast([P, D]))
            const(w1_sb[:, :], w1_t)
            const(b1_sb[:, :], b1.rearrange("(d a) -> d a", a=1))
            const(w2_sb[0:D, :], w2_t)
            const(w2_sb[D:D + 1, :], b2.rearrange("(a d) -> a d", a=1))
            const(emb_sb[:, :], emb)
            const(embt_sb[:, :], emb_t)
            const(adapt_sb[:, :], adapt_t)
            for to, of in ((wide2, weight2), (wide3, weight3)):
                for k in range(2):
                    const(to[k * D:k * D + D, k * D:k * D + D], of)
            assert n[0] == 18

            def begin(k, i, table, first, of, width):
                for j in range(CHUNKS // TRIPS):
                    sync.dma_start(by_chunk(table)[:, bass.ds((CHUNKS // TRIPS * i + j) * C, C), first:first + width],
                                   of[:, 0:width].rearrange("p (a w) -> p a w", a=1).to_broadcast([P, C, width]))\
                        .then_inc(s_zero[k], 16)

            def keyrows(g, v, which):
                for k in which:
                    sync.dma_start(keyrow[:, v % 2, k, :],
                                   (dst_rows, src_rows)[k][:, bass.ds(g * DUMP, DUMP)].to_broadcast([P, DUMP]))\
                        .then_inc(key_in[v % 2], 16)

            sync.wait_ge(s_centred, 1)
            for layer in range(4):
                bulk = BULK_TRIPS * layer
                if layer:
                    sync.wait_ge(s_added, 16 * TILES * layer + START_DMA)
                    for u in range(2):
                        sync.wait_ge(bulk_stored[u], 16 * bulk + START_DMA)
                if layer == 1:
                    sync.wait_ge(s_gstored, 16 * TILES // HALF + START_DMA)
                    sync.wait_ge(s_estored, 16 * TILES // BATCH + START_DMA)

                def chunk(q, u, ii):
                    table = (None, table0_c, table1_c, table2_c)[layer]
                    width = (0, W0, W1, W2)[layer]
                    sync.wait_ge(bulk_used[u], bulk + ii + START)
                    sync.dma_start(bin_[:, u, 0:C * width].rearrange("p (c w) -> p c w", w=width),
                                   table[:, bass.ds(q * C, C), :]).then_inc(bulk_in[u], 16)

                started = ((table1, AGG, zeros, D + 1), (table2, AGG, bias2_b, D), (agg3, 0, bias3_b, D), None)[layer]
                with sync.Fori(0, TRIPS) as i:
                    for kind, k, part in ORDERS[layer][0]:
                        if kind == "count":
                            g = GROUPS * i + k
                            sync.wait_ge(s_counted, (g - 1 if k else g) + START)
                            keyrows(g, k, (0, 1))
                        elif kind == "gate":
                            j = BLOCKS * i + k
                            sync.wait_ge(s_hpre, (j - 1 if k else j) + START)
                            sync.dma_start(attr_sb[k % 2], attr_t[:, bass.ds(j * (HALF * P), HALF * P)])\
                                .then_inc(attr_in[k % 2], 16)
                        elif layer == 1 and kind == "edge" and part == EDGE_PARTS[1][0]:
                            sync.wait_ge(side_used[k], i + START)
                            at = 2 * i + k
                            sync.dma_start(gate_in[:, k, :, :].rearrange("p t d -> p (t d)"),
                                           gates[:, bass.ds(at * (BATCH * D), BATCH * D)]).then_inc(side_in[k], 16)
                            sync.dma_start(emb_in[:, k, :, :].rearrange("p t d -> p (t d)"),
                                           src_emb[:, bass.ds(at * (BATCH * EMB), BATCH * EMB)]).then_inc(side_in[k], 16)
                        if kind == "bulk" and part == BULK_PARTS[layer][0]:
                            chunk(2 * i + k, k, i)
                    if started:
                        begin(layer + 1, i, *started)
                if started:
                    width = (W1, W2, D)[layer]
                    sync.dma_start(started[0][NODES:ROWS, :].rearrange("(p c) w -> p c w", p=P),
                                   zeros[:, 0:width].rearrange("p (a w) -> p a w", a=1).to_broadcast([P, DUMP // P, width]))\
                        .then_inc(s_zero[layer + 1], 16)
                if layer == 0:
                    sync.wait_ge(s_counted, GROUPS * TRIPS + START)
                with sync.Fori(0, TRIPS) as i:
                    for kind, k, part in ORDERS[layer][1]:
                        if kind == "group":
                            g = GROUPS * i + k
                            sync.wait_ge(s_same, (GROUPS * TRIPS * layer + (g - 1 if k else g)) + START)
                            keyrows(g, k, (TO_SRC[layer],))
                        elif kind == "bulk" and part == BULK_PARTS[layer][0]:
                            chunk(BULK_TRIPS + 2 * i + k, k, TRIPS + i)

            bulk = BULK_TRIPS * 4
            sync.wait_ge(s_added, 16 * TILES * 4 + START_DMA)
            for u in range(2):
                sync.wait_ge(bulk_stored[u], 16 * bulk + START_DMA)
            with sync.Fori(0, BULK_TRIPS) as i:
                for u in range(2):
                    sync.wait_ge(bulk_used[u], bulk + i + START)
                    for k, t in ((0, base3_c), (1, agg3_c)):
                        sync.dma_start(bin_[:, u, k * C * D:(k + 1) * C * D].rearrange("p (c d) -> p c d", d=D),
                                       t[:, bass.ds((2 * i + u) * C, C), :]).then_inc((bulk_in, bulk_in2)[k][u], 16)

        @block.gpsimd
        def _(pool):
            steps = [0]

            def step(ins):
                steps[0] += 1
                ins.then_inc(s_pool, 1)
                pool.wait_ge(s_pool, steps[0])

            step(pool.memset(wide2[:, :], 0.0))
            step(pool.memset(wide3[:, :], 0.0))
            step(pool.memset(hidden, 1.0))
            step(pool.memset(turned[:, :], 1.0))
            pool.memset(zeros[:, :], 0.0).then_inc(s_built, 1)
            pool.wait_ge(s_built, 1)
            pool.dma_start(table0[NODES:ROWS, :].rearrange("(p c) w -> p c w", p=P),
                           zeros[:, 0:W0].rearrange("p (a w) -> p a w", a=1).to_broadcast([P, DUMP // P, W0]))\
                .then_inc(s_added, 16)
            step(pool.memset(ident[:, :], 0.0))
            step(pool.affine_select(out=ident[:, :], in_=ident[:, :], compare_op=ALU.not_equal, fill=1.0,
                                    base=0, pattern=[[-1, P]], channel_multiplier=1))
            step(pool.tensor_copy(ident_b[:, :], ident[:, :]))
            step(pool.memset(earlier[:, :], 1.0))
            step(pool.affine_select(out=earlier[:, :], in_=earlier[:, :], compare_op=ALU.is_gt, fill=0.0,
                                    base=DUMP, pattern=[[-1, DUMP + P]], channel_multiplier=1))
            iota = seen_tmp[:, 0:TYPES].bitcast(i32)
            step(pool.iota(iota, pattern=[[1, TYPES]], base=0, channel_multiplier=0))
            step(pool.tensor_copy(type_iota[:, :], iota))
            iota = seen_tmp[:, TYPES:TYPES + TILES].bitcast(i32)
            step(pool.iota(iota.rearrange("p (g j) -> p g j", j=GROUP), pattern=[[0, TILES // GROUP], [P, GROUP]],
                           base=NODES, channel_multiplier=1))
            pool.tensor_copy(dump_row[:, :], iota).then_inc(s_iota, 1)

            pool.wait_ge(s_const, 16 * 18)
            for layer in range(4):
                if layer:
                    pool.wait_ge(s_added, 16 * TILES * layer + START_DMA)
                if layer != 1:
                    for u in range(2):
                        pool.wait_ge(bulk_stored[u], 16 * BULK_TRIPS * max(layer, 1) + START_DMA)
                table = (table0, table0, table1, table2)[layer]
                width = (W0, W0, W1, W2)[layer]
                key = dst_i if TO_SRC[layer] else src_i
                with pool.Fori(0, TRIPS) as i:
                    for u in range(2):
                        pool.wait_ge(rows_used[u], TRIPS * layer + i + START)
                        pool.tensor_copy(row_index[:, u, :], key[:, bass.ds((2 * i + u) * BATCH, BATCH)])\
                            .then_inc(index_in[u], 1)
                        pool.wait_ge(index_in[u], TRIPS * layer + i + 1)
                        apart(pool)
                        for k in range(BATCH):
                            pool.indirect_dma_start(
                                out=rows[:, u, k * width:(k + 1) * width], out_offset=None, in_=table,
                                in_offset=bass.IndirectOffsetOnAxis(ap=row_index[:, u, k:k + 1], axis=0),
                            ).then_inc(rows_in[u], 16)
                for u in range(2):
                    pool.wait_ge(rows_in[u], 16 * BATCH * TRIPS * (layer + 1))
                if layer:
                    pool.wait_ge(s_zero[layer], 16 * (CHUNKS + 1))
                to = (table0, table1, table2, agg3)[layer]
                first = (0, AGG, AGG, 0)[layer]
                width = (W, W, D, D)[layer]
                with pool.Fori(0, TRIPS) as i:
                    for v in range(GROUPS):
                        g = GROUPS * TRIPS * layer + GROUPS * i + v
                        pool.wait_ge(s_staged, g + 1 + START)
                        pool.wait_ge(s_added, 16 * GROUP * g + START_DMA)
                        apart(pool)
                        for k in range(GROUP):
                            pool.indirect_dma_start(
                                out=to, out_offset=bass.IndirectOffsetOnAxis(ap=to_index[:, v % 2, k:k + 1], axis=0),
                                in_=to_add[:, v % 2, k * width:(k + 1) * width], in_offset=None,
                                element_offset=first, compute_op=ALU.add,
                            ).then_inc(s_added, 16)

        @block.scalar
        def _(act):
            with act.Fori(0, BULK_TRIPS) as i:
                for u in range(2):
                    act.wait_ge(bulk_out[u], i + 1)
                    act.dma_start(table0_c[:, bass.ds((2 * i + u) * C, C), :],
                                  bout[:, u, :].rearrange("p (c w) -> p c w", w=W0)).then_inc(bulk_stored[u], 16)
            act.wait_ge(s_adapt, 1)
            act.activation(adapted[:, :], ps_gate[0:TYPES, 0:EMB], ACT.Copy).then_inc(s_adapted, 1)
            act.wait_ge(s_const, 16 * 18)

            def group(layer, i, v):
                g = GROUPS * TRIPS * layer + GROUPS * i + v
                width = (W, W, D, D)[layer]
                to = src_to if TO_SRC[layer] else dst_to
                act.wait_ge(s_summed, g + 1 + START)
                act.wait_ge(s_added, 16 * GROUP * (g - 1 if v else g) + START_DMA)
                act.activation(to_index[:, v % 2, :], to[:, bass.ds((GROUPS * i + v) * GROUP, GROUP)], ACT.Copy)
                act.activation(to_add[:, v % 2, 0:GROUP * width], ps_sum[v % 2][:, 0:GROUP * width], ACT.Copy)\
                    .then_inc(s_staged, 1)

            def gate(i, w):
                n = BLOCKS * i + w
                act.wait_ge(s_hpre, n + 1 + START)
                act.wait_ge(s_gpre, n + START)
                act.activation(hidden[0:D, :].rearrange("p (b n) -> p b n", b=2),
                               ps_turn[0:D, :].rearrange("p (b n) -> p b n", b=2)[:, :, 0:HALF * P // 2],
                               ACT.Silu, bias=b1_sb[:, :]).then_inc(s_hid, 1)
                act.wait_ge(s_gpre, n + 1 + START)
                act.wait_ge(s_gstored, 16 * n + START_DMA)
                act.activation(gate_out, ps_gate[:, 0:HALF * D].rearrange("p (t d) -> p t d", d=D), ACT.Copy).then_inc(s_gate, 1)
                act.wait_ge(s_gate, n + 1 + START)
                act.dma_start(gates[:, bass.ds(n * (HALF * D), HALF * D)], gate_out.rearrange("p t d -> p (t d)"))\
                    .then_inc(s_gstored, 16)

            def square(state, squared, n, dev, sq):
                act.wait_ge(state, n)
                act.activation(sq, dev, ACT.Square).then_inc(squared, 1)

            def root(ready, done, n, var, std):
                act.wait_ge(ready, n + 1)
                act.activation(std, var, ACT.Sqrt, bias=eps[:, :], scale=1.0 / D).then_inc(done, 1)

            def turn_copy(n):
                act.wait_ge(s_turned, n + 1)
                act.activation(turned[0:2 * D, :], ps_turn[0:2 * D, 0:PAIRS * P], ACT.Copy).then_inc(s_turnc, 1)

            def hot_copy(n):
                act.wait_ge(s_hott, n + 1 + START)
                act.wait_ge(s_look, n + START)
                act.activation(hot_turned[0:TYPES, :], ps_hot[0:TYPES, 0:BATCH * P], ACT.Copy).then_inc(s_hotc, 1)

            def edge(layer, i, u, part):
                b = 2 * i + u
                n = EDGE_NORMS[layer] + i * (2 if layer == 2 else 1)
                tiles = bass.ds(b * BATCH, BATCH)
                dev, sq = edev[:, u, :, :], esq[:, u, :, :]
                if part == "hot":
                    width = W0
                    square(rows_in[u], e_sqd[u], 16 * BATCH * (TRIPS * layer + i + 1),
                           rows[:, u, 0:BATCH * width].rearrange("p (t w) -> p t w", w=width)[:, :, 0:D], sq)
                    hot_copy(TILES // BATCH + b)
                elif part in ("rescale", "sum"):
                    square(e_dev[u], e_sqd[u], n - EDGE_NORMS[2] + 1, dev, sq)
                elif part == "var":
                    root(e_var[u], e_std[u], n, evar[:, u, :], estd[:, u, :])
                    if layer == 3:
                        act.wait_ge(s_deg[u], i + 1)
                        act.activation(efac[:, u, :], efac[:, u, :], ACT.Sqrt, bias=zero1[:, :]).then_inc(s_degroot[u], 1)
                elif part == "gamma":
                    turn_copy(product_number(layer, 0, i, ("edge", u, part)))
                    act.wait_ge(e_dev[u], n - EDGE_NORMS[2] + 2)
                    act.activation(dev, sq, ACT.Square).then_inc(e_sqd[u], 1)
                elif part == "var2":
                    root(e_var[u], e_std[u], n + 1, evar[:, u, :], estd[:, u, :])
                elif part == "weight":
                    m = product_number(layer, 0, i, ("edge", u, part))
                    turn_copy(m)
                    act.wait_ge(s_prod, m + 1)
                    act.wait_ge(s_parts[u], 2 * (TRIPS * layer + i) + START)
                    act.activation(emsg[:, u, :, 0:D].rearrange("p (q k) d -> p q k d", k=2),
                                   ps_prod[:, 0:PAIRS * P].rearrange("p (q n) -> p q n", n=P)[:, :, 0:2 * D]
                                   .rearrange("p q (k d) -> p q k d", k=2), ACT.Copy).then_inc(s_taken, 1)
                    act.wait_ge(s_taken, m + 1 + START)
                elif part == "split":
                    done = TRIPS * layer + i
                    for k, (ready, of) in enumerate(((s_msg, emsg), (s_rest, erest))):
                        if k or layer < 2:
                            act.wait_ge(ready[u], (done if k or layer < 2 else 0) + 1)
                        act.activation(parts[:, tiles, k, :], top_half(of[:, u, :, :].rearrange("p t w -> p (t w)"))
                                       .rearrange("p (t w) -> p t w", w=W), ACT.Copy).then_inc(s_parts[u], 1)

            def bulk(layer, phase, i, u, part):
                q, ii = BULK_TRIPS * phase + 2 * i + u, TRIPS * phase + i
                n = BULK_NORMS[layer] + ii * (2 if layer == 2 else 1)
                dev, sq = bdev[:, u, :, :], bsq[:, u, :, :]
                if part == "square":
                    square(bulk_in[u], b_sqd[u], 16 * (BULK_TRIPS * layer + ii + 1),
                           bin_[:, u, 0:C * W0].rearrange("p (c w) -> p c w", w=W0)[:, :, 0:D], sq)
                elif part in ("rescale", "sum"):
                    square(b_dev[u], b_sqd[u], n - BULK_NORMS[2] + 1, dev, sq)
                elif part == "var":
                    root(b_var[u], b_std[u], n, bvar[:, u, :], bstd[:, u, :])
                elif part in ("gamma0", "gamma1", "mm0", "mm1"):
                    turn_copy(product_number(layer, phase, i, ("bulk", u, part)))
                    if part == "gamma1":
                        act.wait_ge(b_dev[u], n - BULK_NORMS[2] + 2)
                        act.activation(dev, sq, ACT.Square).then_inc(b_sqd[u], 1)
                elif part == "var2":
                    root(b_var[u], b_std[u], n + 1, bvar[:, u, :], bstd[:, u, :])
                if part == BULK_PARTS[layer][-1]:
                    width = (0, D + 1, D + 1, D)[layer]
                    act.wait_ge(bulk_out[u], BULK_TRIPS * layer + ii + 1)
                    act.dma_start((None, table1_c, table2_c, base3_c)[layer][:, bass.ds(q * C, C), 0:width],
                                  bout[:, u, 0:C * width].rearrange("p (c w) -> p c w", w=width)).then_inc(bulk_stored[u], 16)

            act.wait_ge(s_built, 1)
            act.dma_start(gates[:, 0:D], zeros[:, 0:D]).then_inc(s_gstored, 16)
            act.dma_start(src_emb[:, 0:EMB], zeros[:, 0:EMB]).then_inc(s_estored, 16)
            for layer in range(4):
                with act.Fori(0, TRIPS) as i:
                    for kind, u, part in ORDERS[layer][0]:
                        if kind == "edge":
                            edge(layer, i, u, part)
                        elif kind == "bulk":
                            bulk(layer, 0, i, u, part)
                        elif kind == "gate":
                            gate(i, u)
                if layer == 0:
                    act.wait_ge(s_ready, 1)
                    act.activation(cw[:, :], cw[:, :], ACT.Sin, bias=half_pi[:, :], scale=-math.pi / 12).then_inc(s_ready, 1)
                    act.wait_ge(s_ready, 2)
                    act.activation(cw[:, :], cw[:, :], ACT.Square).then_inc(s_ready, 1)
                with act.Fori(0, TRIPS) as i:
                    for kind, k, part in ORDERS[layer][1]:
                        if kind == "group":
                            group(layer, i, k)
                        elif kind == "bulk":
                            bulk(layer, 1, i, k, part)
                        elif part == "hot":
                            hot_copy(2 * i + k)
                        else:
                            n = 2 * i + k
                            act.wait_ge(s_look, n + 1 + START)
                            act.wait_ge(s_estored, 16 * n + START_DMA)
                            act.activation(looked[:, :, :], ps_look[:, 0:BATCH * EMB].rearrange("p (t d) -> p t d", d=EMB),
                                           ACT.Copy).then_inc(s_looked, 1)
                            act.wait_ge(s_looked, n + 1 + START)
                            act.dma_start(src_emb[:, bass.ds(n * (BATCH * EMB), BATCH * EMB)],
                                          looked[:, :, :].rearrange("p t d -> p (t d)")).then_inc(s_estored, 16)
            with act.Fori(0, BULK_TRIPS) as i:
                n = BULK_NORMS[4] + i
                for u in range(2):
                    square(b_dev[u], b_sqd[u], n - BULK_NORMS[2] + 1, bdev[:, u, :, :], bsq[:, u, :, :])
                for u in range(2):
                    root(b_var[u], b_std[u], n, bvar[:, u, :], bstd[:, u, :])
                for u in range(2):
                    act.wait_ge(bulk_out[u], BULK_TRIPS * 4 + i + 1)
                    act.dma_start(out_c[:, bass.ds((2 * i + u) * C, C), :],
                                  bout[:, u, 0:C * D].rearrange("p (c d) -> p c d", d=D)).then_inc(bulk_stored[u], 16)
            for u in range(2):
                act.wait_ge(bulk_stored[u], 16 * BULK_TRIPS * 5 + START_DMA)

        @block.tensor
        def _(pe):
            pe.wait_ge(s_const, 16 * 18)
            pe.wait_ge(s_iota, 1)
            pe.matmul(ps_gate[0:TYPES, 0:EMB], lhsT=embt_sb[:, :], rhs=adapt_sb[:, :], start=True, stop=True)\
                .then_inc(s_adapt, 1)
            pe.wait_ge(s_adapted, 1)

            def gate(i, w):
                n = BLOCKS * i + w
                pe.wait_ge(attr_in[w % 2], 16 * (BLOCKS // 2 * i + w // 2 + 1))
                pe.wait_ge(s_hid, n + START)
                apart(pe)
                for k in range(2):
                    last = pe.matmul(ps_turn[0:D, k * 512:k * 512 + HALF * P // 2], lhsT=w1_sb[:, :],
                                     rhs=attr_sb[w % 2][:, k * HALF * P // 2:(k + 1) * HALF * P // 2], start=True, stop=True)
                last.then_inc(s_hpre, 1)
                pe.wait_ge(s_hid, n + 1 + START)
                pe.wait_ge(s_gate, n + START)
                for k in range(HALF):
                    last = pe.matmul(ps_gate[:, k * D:(k + 1) * D], lhsT=hidden[0:D + 1, k * P:(k + 1) * P],
                                     rhs=w2_sb[:, :], start=True, stop=True)
                last.then_inc(s_gpre, 1)

            def group(layer, i, v):
                g = GROUPS * TRIPS * layer + GROUPS * i + v
                width = (W, W, D, D)[layer]
                pe.wait_ge(s_same, g + 1 + START)
                pe.wait_ge(s_staged, (g - 1 if v else g) + START)
                for to in range(GROUP):
                    for of in range(GROUP):
                        for k in range(3):
                            last = pe.matmul(ps_sum[v % 2][:, to * width:(to + 1) * width],
                                             lhsT=same[:, v % 2, of, to * P:(to + 1) * P],
                                             rhs=parts[:, bass.ds((GROUPS * i + v) * GROUP + of, 1), k, 0:width]
                                             .rearrange("p a w -> p (a w)"),
                                             start=(of == k == 0), stop=(of == GROUP - 1 and k == 2))
                last.then_inc(s_summed, 1)

            def lookup(n, table):
                pe.wait_ge(s_hot, n + 1)
                pe.wait_ge(s_hotc, n + START)
                for t in range(BATCH):
                    last = pe.transpose(ps_hot[0:TYPES, t * P:(t + 1) * P], onehot[:, t, :], ident_b[:, :])
                last.then_inc(s_hott, 1)
                pe.wait_ge(s_hotc, n + 1 + START)
                pe.wait_ge(s_looked, n + START)
                for t in range(BATCH):
                    for k in range(3):
                        last = pe.matmul(ps_look[:, t * EMB:(t + 1) * EMB], lhsT=hot_turned[0:TYPES, t * P:(t + 1) * P],
                                         rhs=table[:, k, :], start=(k == 0), stop=(k == 2))
                last.then_inc(s_look, 1)

            def product(n, of, weights, rows_):
                for q in range(PAIRS):
                    last = pe.transpose(ps_turn[0:2 * D, q * P:(q + 1) * P], of[:, q * 2 * D:(q + 1) * 2 * D], ident[:, :])
                last.then_inc(s_turned, 1)
                pe.wait_ge(s_turnc, n + 1)
                pe.wait_ge(s_taken, n + START)
                for q in range(PAIRS):
                    last = pe.matmul(ps_prod[:, q * P:q * P + 2 * D], lhsT=turned[0:rows_, q * P:(q + 1) * P],
                                     rhs=weights[:, :], start=True, stop=True)
                last.then_inc(s_prod, 1)

            for layer in range(4):
                for phase in range(2):
                    with pe.Fori(0, TRIPS) as i:
                        for item in ORDERS[layer][phase]:
                            kind, u, part = item
                            if kind == "group":
                                group(layer, i, u)
                            elif kind == "gate":
                                gate(i, u)
                            elif part == "hot":
                                if kind == "look":
                                    lookup(2 * i + u, emb_parts)
                                else:
                                    lookup(TILES // BATCH + 2 * i + u, adapted_parts)
                            elif part in PRODUCTS:
                                n = product_number(layer, phase, i, item)
                                if kind == "edge":
                                    inputs = EDGE_INPUTS[layer] + (2 * i + (part == "weight") if layer == 2 else i)
                                    pe.wait_ge(e_input[u], inputs + 1)
                                    of = edev[:, u, :, :].rearrange("p t d -> p (t d)")
                                else:
                                    pe.wait_ge(b_input[u], BULK_INPUTS[layer] + TRIPS * phase + i + 1)
                                    of = bdev[:, u, :, :].rearrange("p t d -> p (t d)")
                                    h = int(part[-1])
                                    of = of[:, h * BATCH * D:(h + 1) * BATCH * D]
                                if part.startswith("gamma"):
                                    product(n, of, wide_gamma, 2 * D + 1)
                                else:
                                    product(n, of, (wide2, wide3)[layer - 2], 2 * D)
                    if phase == 0:
                        for u in range(2):
                            pe.wait_ge(s_parts[u], 2 * TRIPS * (layer + 1) + START)

        @block.vector
        def _(dve):
            class Steps:
                base, k, i, per = 0, 0, None, 0

                def __call__(self, ins):
                    ins.then_inc(s_step, 1)
                    self.k += 1
                    done = self.base + self.k
                    dve.wait_ge(s_step, done if self.i is None else self.i * self.per + done)

            step = Steps()

            @contextmanager
            def loop(trips, per):
                with dve.Fori(0, trips) as i:
                    step.base, step.k, step.i, step.per = step.base + step.k, 0, i, per
                    yield i
                    assert step.k == per, step.k
                step.base, step.k, step.i = step.base + trips * per, 0, None

            def over(stat, k):
                return stat.rearrange("p (t a) -> p t a", a=1).to_broadcast([P, k, D])

            def column(row, k):
                return row[:, :, k:k + 1].rearrange("p t a -> p (t a)")

            def pairs(prod):
                return prod[:, 0:PAIRS * P].rearrange("p (q n) -> p q n", n=P)[:, :, 0:2 * D].rearrange("p q (k d) -> p q k d", k=2)

            def by_pair(t):
                return t.rearrange("p (q k) d -> p q k d", k=2)

            dve.memset(eps[:, :], EPS)
            dve.memset(half_pi[:, :], math.pi / 2)
            dve.memset(emsg[:, :, :, D:W], 1.0)
            step(dve.memset(zero1[:, :], 0.0))
            step(dve.memset(bout[:, :, :], 0.0))
            for u in range(2):
                dve.wait_ge(bulk_stored[u], START_DMA)
            mult_c = mult_in[:, :].rearrange("p (c a) -> p c a", a=1)
            type_c = type_in[:, :].rearrange("p (c a) -> p c a", a=1)
            with loop(BULK_TRIPS, PER_FIRST) as i:
                for u in range(2):
                    o = bout[:, u, :].rearrange("p (c w) -> p c w", w=W0)
                    of = bin_[:, u, 0:C * D].rearrange("p (c d) -> p c d", d=D)
                    at = bass.ds((2 * i + u) * C, C)
                    dve.wait_ge(bulk_in[u], 16 * i + 16)
                    step(dve.reduce_sum(bvar[:, u, :], of, AX.X))
                    dve.wait_ge(bulk_stored[u], 16 * i + START_DMA)
                    dve.scalar_tensor_tensor(o[:, :, 0:D], over(bvar[:, u, :], C), -1.0 / D, of, ALU.mult, ALU.add)\
                        .then_inc(bulk_used[u], 1)
                    dve.tensor_copy(o[:, :, MULT:MULT + 1], mult_c[:, at, :])
                    dve.tensor_copy(o[:, :, TYPE:TYPE + 1], type_c[:, at, :]).then_inc(bulk_out[u], 1)
            dve.wait_ge(s_const, 16 * 18)
            dve.wait_ge(s_iota, 1)
            step(dve.tensor_copy(src_f[:, :], src_i[:, :]))
            step(dve.tensor_copy(dst_f[:, :], dst_i[:, :]))
            dve.tensor_scalar(cw[:, :], ew[:, :], 6.0, None, ALU.min).then_inc(s_ready, 1)
            step(dve.tensor_tensor(wide_gamma[0:2 * D, :].rearrange("p (k d) -> p k d", k=2),
                                   ident[0:2 * D, 0:2 * D].rearrange("p (k d) -> p k d", k=2),
                                   gamma_b[0:2 * D, :].rearrange("p (k d) -> p k d", k=1).to_broadcast([2 * D, 2, D]), ALU.mult))
            step(dve.tensor_copy(wide_gamma[2 * D:2 * D + 1, :].rearrange("p (k d) -> p k d", k=2),
                                 beta_b[2 * D:2 * D + 1, :].rearrange("p (k d) -> p k d", k=1).to_broadcast([1, 2, D])))
            for t, k in ((wide_gamma, 2), (wide2, 2), (wide3, 2), (bias2_b, 1), (bias3_b, 1)):
                blocks = t[:, :].rearrange("p (k d) -> p k d", k=k)
                p = t.shape[0]
                mean = wide_mean[0:p, 0:k]
                step(dve.reduce_sum(mean, blocks, AX.X))
                ins = dve.scalar_tensor_tensor(blocks, mean.rearrange("p (k a) -> p k a", a=1).to_broadcast([p, k, D]),
                                               -1.0 / D, blocks, ALU.mult, ALU.add)
                if t is bias3_b:
                    ins.then_inc(s_centred, 1)
                else:
                    step(ins)
            dve.wait_ge(s_adapted, 1)
            for t, to in ((emb_sb, emb_parts), (adapted, adapted_parts)):
                step(dve.tensor_copy(to[:, 0, :], top_half(t[:, :])))
                step(dve.tensor_tensor(emb_rest[:, :], t[:, :], to[:, 0, :], ALU.subtract))
                step(dve.tensor_copy(to[:, 1, :], top_half(emb_rest[:, :])))
                step(dve.tensor_tensor(to[:, 2, :], emb_rest[:, :], to[:, 1, :], ALU.subtract))

            same_key = (dst_f, src_f, src_f, dst_f)

            def count(i, v):
                g = GROUPS * i + v
                per = 4 if v % 2 == 0 else 3
                dve.wait_ge(key_in[v % 2], i * (per * 32) + (v // 2 + 1) * 32)
                for k, (key, seen) in enumerate(((dst_f, dst_seen), (src_f, src_seen))):
                    for j in range(GROUP):
                        at = bass.ds(g * GROUP + j, 1)
                        last = dve.scalar_tensor_tensor(
                            seen_tmp[:, 0:(j + 1) * P], keyrow[:, v % 2, k, 0:(j + 1) * P], key[:, at],
                            earlier[:, DUMP - j * P:DUMP + P], ALU.is_equal, ALU.mult, accum_out=seen[:, at])
                        if k == 0 or j < GROUP - 1:
                            step(last)
                last.then_inc(s_counted, 1)
                dve.wait_ge(s_counted, g + 1 + START)

            def group(layer, i, v):
                g = GROUPS * TRIPS * layer + GROUPS * i + v
                per = 4 if v % 2 == 0 else 3
                before = TRIPS * per * (32 + 16 * layer)
                dve.wait_ge(key_in[v % 2], before + i * (per * 16) + (v // 2 + 1) * 16)
                dve.wait_ge(s_summed, (g - 1 if v else g) + START)
                for j in range(GROUP):
                    last = dve.tensor_scalar(same[:, v % 2, j, :], keyrow[:, v % 2, TO_SRC[layer], :],
                                             same_key[layer][:, bass.ds((GROUPS * i + v) * GROUP + j, 1)], None, ALU.is_equal)
                last.then_inc(s_same, 1)

            def hot(n, types):
                dve.wait_ge(s_hott, n + START)
                dve.tensor_tensor(onehot[:, :, :],
                                  type_iota[:, :].rearrange("p (a n) -> p a n", a=1).to_broadcast([P, BATCH, TYPES]),
                                  types.to_broadcast([P, BATCH, TYPES]), ALU.is_equal).then_inc(s_hot, 1)

            def variance(squared, n, sq, var, ready):
                dve.wait_ge(squared, n + 1)
                dve.reduce_sum(var, sq, AX.X).then_inc(ready, 1)

            def inverse(std, done, n, free=None):
                dve.wait_ge(done, n + 1)
                ins = dve.reciprocal(std, std)
                if free:
                    ins.then_inc(free[0], 1)
                    dve.wait_ge(*free)
                else:
                    step(ins)

            def rescale(row, dev, fac, k, ready):
                step(dve.tensor_scalar(fac, column(row, TOT), 1e-8, None, ALU.max))
                step(dve.reciprocal(fac, fac))
                step(dve.tensor_tensor(dev, row[:, :, AGG:AGG + D], over(fac, k), ALU.mult))
                dve.tensor_tensor(dev, dev, row[:, :, 0:D], ALU.add).then_inc(ready, 1)

            def edge(layer, i, u, part):
                b = 2 * i + u
                width = (W0, W0, W1, W2)[layer]
                row = rows[:, u, 0:BATCH * width].rearrange("p (t w) -> p t w", w=width)
                tiles = bass.ds(b * BATCH, BATCH)
                n = EDGE_NORMS[layer] + i * (2 if layer == 2 else 1)
                done = TRIPS * layer + i
                dev, sq, msg, rest = edev[:, u, :, :], esq[:, u, :, :], emsg[:, u, :, :], erest[:, u, :, :]
                var, std, fac, fac2 = evar[:, u, :], estd[:, u, :], efac[:, u, :], efac2[:, u, :]
                if part == EDGE_PARTS[layer][0]:
                    dve.wait_ge(rows_in[u], 16 * BATCH * (done + 1))
                if part == "split":
                    flat_msg, flat_rest = (t.rearrange("p t w -> p (t w)") for t in (msg, rest))
                    if layer < 2:
                        dve.wait_ge(s_msg[u], done + 1)
                    else:
                        dve.wait_ge(s_taken, product_number(layer, 0, i, ("edge", u, "weight")) + 1 + START)
                        dve.wait_ge(s_parts[u], 2 * done + START)
                    dve.tensor_tensor(flat_rest, flat_msg, top_half(flat_msg), ALU.subtract).then_inc(s_rest[u], 1)
                    dve.wait_ge(s_rest[u], done + 1)
                    dve.tensor_tensor(parts[:, tiles, 2, :], rest, top_half(flat_rest).rearrange("p (t w) -> p t w", w=W),
                                      ALU.subtract)
                elif layer == 0:
                    dve.wait_ge(s_parts[u], 2 * done + START)
                    dve.tensor_tensor(msg[:, :, 0:D], row[:, :, 0:D], over(ew[:, tiles], BATCH), ALU.mult).then_inc(s_msg[u], 1)
                    dve.tensor_copy(src_type[:, tiles], column(row, TYPE)).then_inc(rows_used[u], 1)
                elif part == "hot":
                    hot(TILES // BATCH + b, row[:, :, TYPE:TYPE + 1])
                elif part == "rescale":
                    rescale(row, dev, fac, BATCH, e_dev[u])
                elif part == "sum":
                    dve.tensor_tensor(dev, row[:, :, 0:D], row[:, :, AGG:AGG + D], ALU.add).then_inc(e_dev[u], 1)
                    step(dve.tensor_scalar(fac2, dst_deg[:, tiles], 1.0, None, ALU.add))
                    dve.scalar_tensor_tensor(fac, column(row, DEG), 1.0, fac2, ALU.add, ALU.mult).then_inc(s_deg[u], 1)
                elif part in ("var", "var2"):
                    variance(e_sqd[u], n + (part == "var2"), dev if part == "var2" else sq, var, e_var[u])
                elif part == "norm":
                    inverse(std, e_std[u], n)
                    ins = dve.tensor_tensor(dev, dev if layer == 2 else row[:, :, 0:D], over(std, BATCH), ALU.mult)
                    if layer == 2:
                        ins.then_inc(e_input[u], 1)
                    else:
                        step(ins)
                elif part == "gamma":
                    m = product_number(layer, 0, i, ("edge", u, part))
                    dve.wait_ge(s_prod, m + 1)
                    dve.tensor_tensor(by_pair(sq), pairs(ps_prod), by_pair(row[:, :, 0:D]), ALU.add).then_inc(s_taken, 1)
                    dve.wait_ge(s_taken, m + 1 + START)
                    dve.tensor_copy(fac2, std).then_inc(e_dev[u], 1)
                elif part == "scale":
                    if layer == 2:
                        inverse(std, e_std[u], n + 1, (rows_used[u], done + 1 + START))
                        step(dve.tensor_tensor(fac, std, ew[:, tiles], ALU.mult))
                        dve.tensor_tensor(dev, sq, over(fac, BATCH), ALU.mult).then_inc(e_input[u], 1)
                    else:
                        dve.wait_ge(s_degroot[u], i + 1)
                        step(dve.reciprocal(fac, fac))
                        inverse(std, e_std[u], n, (rows_used[u], done + 1 + START))
                        step(dve.tensor_tensor(fac, fac, std, ALU.mult))
                        dve.tensor_tensor(dev, dev, over(fac, BATCH), ALU.mult).then_inc(e_input[u], 1)
                elif part == "logit":
                    dve.wait_ge(s_look, TILES // BATCH + b + 1 + START)
                    dve.wait_ge(side_in[u], 32 * (i + 1))
                    dve.tensor_tensor(emb_in[:, u, :, :], ps_look[:, 0:BATCH * EMB].rearrange("p (t d) -> p t d", d=EMB),
                                      emb_in[:, u, :, :], ALU.mult).then_inc(s_looked, 1)
                    dve.wait_ge(s_looked, TILES // BATCH + b + 1 + START)
                    step(dve.reduce_sum(logit[:, u, :], emb_in[:, u, :, :], AX.X))
                elif part == "message" and layer == 1:
                    gate = gate_in[:, u, :, :]
                    dve.tensor_copy(dst_deg[:, tiles], column(row, DEG))
                    dve.wait_ge(s_parts[u], 2 * done + START)
                    dve.tensor_copy(msg[:, :, D:W], row[:, :, MULT:MULT + 1])
                    dve.tensor_tensor(fac, cw[:, tiles], column(row, MULT), ALU.mult).then_inc(rows_used[u], 1)
                    step(dve.tensor_tensor(gate, gate, over(logit[:, u, :], BATCH), ALU.add))
                    step(dve.tensor_tensor(gate, gate, dev, ALU.mult))
                    dve.wait_ge(rows_used[u], done + 1 + START)
                    dve.tensor_tensor(dev, gate, over(fac, BATCH), ALU.mult).then_inc(side_used[u], 1)
                    dve.wait_ge(side_used[u], i + 1 + START)
                    step(dve.reduce_sum(fac2, dev, AX.X))
                    dve.scalar_tensor_tensor(msg[:, :, 0:D], over(fac2, BATCH), -1.0 / D, dev, ALU.mult, ALU.add)\
                        .then_inc(s_msg[u], 1)

            def bulk(layer, phase, i, u, part):
                ii = TRIPS * phase + i
                width = (0, W0, W1, W2, D)[layer]
                row = bin_[:, u, 0:C * width].rearrange("p (c w) -> p c w", w=width)
                wo = (0, D + 1, D + 1, D, D)[layer]
                o = bout[:, u, 0:C * wo].rearrange("p (c w) -> p c w", w=wo)
                n = BULK_NORMS[layer] + ii * (2 if layer == 2 else 1)
                done = BULK_TRIPS * layer + ii
                dev, sq, var, std, fac = bdev[:, u, :, :], bsq[:, u, :, :], bvar[:, u, :], bstd[:, u, :], bfac[:, u, :]
                free = (bulk_used[u], done + 1 + START)
                if part in ("rescale", "sum"):
                    dve.wait_ge(bulk_in[u], 16 * (done + 1))
                    if layer == 2:
                        rescale(row, dev, fac, C, b_dev[u])
                    elif layer == 3:
                        step(dve.tensor_scalar(fac, column(row, DEG), 1.0, None, ALU.add))
                        step(dve.reciprocal(fac, fac))
                        dve.tensor_tensor(dev, row[:, :, 0:D], row[:, :, AGG:AGG + D], ALU.add).then_inc(b_dev[u], 1)
                    else:
                        dve.wait_ge(bulk_in2[u], 16 * (ii + 1))
                        dve.wait_ge(bulk_out[u], done)
                        sums = bin_[:, u, C * D:2 * C * D].rearrange("p (c d) -> p c d", d=D)
                        dve.tensor_tensor(dev, row, sums, ALU.add).then_inc(b_dev[u], 1)
                elif part in ("var", "var2"):
                    variance(b_sqd[u], n + (part == "var2"), dev if part == "var2" else sq, var, b_var[u])
                elif part == "norm":
                    if layer in (1, 4):
                        dve.wait_ge(bulk_stored[u], 16 * done + START_DMA)
                    if layer == 1:
                        dve.tensor_copy(o[:, :, D:D + 1], row[:, :, DEG:DEG + 1])
                        inverse(std, b_std[u], n)
                        dve.tensor_tensor(o[:, :, 0:D], row[:, :, 0:D], over(std, C), ALU.mult).then_inc(bulk_out[u], 1)
                        dve.wait_ge(bulk_out[u], done + 1)
                        dve.tensor_copy(fac, std).then_inc(bulk_used[u], 1)
                    elif layer == 2:
                        inverse(std, b_std[u], n)
                        dve.tensor_tensor(dev, dev, over(std, C), ALU.mult).then_inc(b_input[u], 1)
                    else:
                        inverse(std, b_std[u], n, free)
                        to, signal = (dev, b_input[u]) if layer == 3 else (o, bulk_out[u])
                        dve.tensor_tensor(to, dev, over(std, C), ALU.mult).then_inc(signal, 1)
                elif part in ("gamma0", "gamma1"):
                    h = int(part[-1])
                    m = product_number(layer, phase, i, ("bulk", u, part))
                    tiles = slice(h * BATCH, (h + 1) * BATCH)
                    dve.wait_ge(s_prod, m + 1)
                    dve.tensor_tensor(by_pair(sq[:, tiles, :]), pairs(ps_prod), by_pair(row[:, tiles, 0:D]), ALU.add)\
                        .then_inc(s_taken, 1)
                    if h:
                        dve.wait_ge(bulk_stored[u], 16 * done + START_DMA)
                        dve.wait_ge(s_taken, m + 1 + START)
                        dve.tensor_copy(o[:, :, D:D + 1], row[:, :, DEG:DEG + 1]).then_inc(b_dev[u], 1)
                elif part == "norm2":
                    inverse(std, b_std[u], n + 1, free)
                    dve.tensor_tensor(o[:, :, 0:D], sq, over(std, C), ALU.mult).then_inc(bulk_out[u], 1)
                elif part in ("mm0", "mm1"):
                    h = int(part[-1])
                    m = product_number(layer, phase, i, ("bulk", u, part))
                    tiles = slice(h * BATCH, (h + 1) * BATCH)
                    if h == 0:
                        dve.wait_ge(bulk_stored[u], 16 * done + START_DMA)
                    dve.wait_ge(s_prod, m + 1)
                    scale = fac[:, tiles].rearrange("p (q k a) -> p q k a", k=2, a=1).to_broadcast([P, PAIRS, 2, D])
                    dve.tensor_tensor(by_pair(o[:, tiles, :]), pairs(ps_prod), scale, ALU.mult).then_inc(s_taken, 1)
                    dve.wait_ge(s_taken, m + 1 + START)
                    ins = dve.tensor_tensor(o[:, tiles, :], o[:, tiles, :], dev[:, tiles, :], ALU.add)
                    if h:
                        ins.then_inc(bulk_out[u], 1)

            for layer in range(4):
                if layer == 1:
                    dve.wait_ge(s_gate, TILES // HALF + START)
                    dve.wait_ge(s_ready, 3)
                with loop(TRIPS, PER_GATHER[layer]) as i:
                    for kind, u, part in ORDERS[layer][0]:
                        if kind == "count":
                            count(i, u)
                        elif kind == "edge":
                            edge(layer, i, u, part)
                        elif kind == "bulk":
                            bulk(layer, 0, i, u, part)
                if layer == 0:
                    for key, seen, to in ((dst_f, dst_seen, dst_to), (src_f, src_seen, src_to)):
                        tmp = seen_tmp[:, 0:TILES]
                        step(dve.tensor_scalar(seen[:, :], seen[:, :], 1.0, None, ALU.min))
                        step(dve.tensor_tensor(tmp, dump_row[:, :], key[:, :], ALU.subtract))
                        step(dve.tensor_tensor(tmp, tmp, seen[:, :], ALU.mult))
                        step(dve.tensor_tensor(to[:, :], key[:, :], tmp, ALU.add))
                with loop(TRIPS, PER_SCATTER[layer]) as i:
                    for kind, k, part in ORDERS[layer][1]:
                        if kind == "group":
                            group(layer, i, k)
                        elif kind == "bulk":
                            bulk(layer, 1, i, k, part)
                        elif part == "hot":
                            hot(2 * i + k, src_type[:, bass.ds((2 * i + k) * BATCH, BATCH)].rearrange("p (t a) -> p t a", a=1))
            with loop(BULK_TRIPS, PER_LAST) as i:
                for part in ("sum", "var", "norm"):
                    for u in range(2):
                        bulk(4, 0, i, u, part)


_PADDED = EDGES - E


def kernel(x, src, dst, edge_attr_40, edge_weight, node_type_119, node_vec, L1_gnn_W1, L1_gnn_b1, L1_gnn_W2,
           L1_gnn_b2, L1_gnn_emb, L1_gnn_adaptW, L1_gnn_gamma, L1_gnn_beta, L2_gnn_weight, L2_gnn_bias,
           L3_gnn_W, L3_gnn_b):
    import numpy as np
    import concourse.bacc as bacc
    from concourse.bass_utils import run_bass_kernel_spmd

    def padded(a, n):
        out = np.zeros((n, *a.shape[1:]), a.dtype)
        out[:len(a)] = a
        return out

    def edge_keys(a):
        return np.concatenate([a, np.arange(N, N + _PADDED, dtype=a.dtype)])

    def tiles(a):
        return np.ascontiguousarray(a.reshape(TILES, P).T)

    t = np.ascontiguousarray
    src, dst = edge_keys(np.asarray(src)), edge_keys(np.asarray(dst))
    arrays = {
        "x": padded(np.asarray(x), NODES), "node_mult": padded(np.asarray(node_vec), NODES),
        "node_type": padded(np.asarray(node_type_119), NODES),
        "src_rows": src.reshape(1, EDGES), "dst_rows": dst.reshape(1, EDGES),
        "src_tiles": tiles(src), "dst_tiles": tiles(dst),
        "attr_t": t(padded(np.asarray(edge_attr_40), EDGES).T), "weight_tiles": tiles(padded(np.asarray(edge_weight), EDGES)),
        "w1_t": t(np.asarray(L1_gnn_W1).T), "b1": np.asarray(L1_gnn_b1), "w2_t": t(np.asarray(L1_gnn_W2).T),
        "b2": np.asarray(L1_gnn_b2), "emb": np.asarray(L1_gnn_emb), "emb_t": t(np.asarray(L1_gnn_emb).T),
        "adapt_t": t(np.asarray(L1_gnn_adaptW).T), "gamma": np.asarray(L1_gnn_gamma), "beta": np.asarray(L1_gnn_beta),
        "weight2": np.asarray(L2_gnn_weight), "bias2": np.asarray(L2_gnn_bias),
        "weight3": np.asarray(L3_gnn_W), "bias3": np.asarray(L3_gnn_b),
    }
    nc = bacc.Bacc("TRN2", target_bir_lowering=False, num_devices=1)
    args = {n: nc.dram_tensor(n, a.shape, mybir.dt.from_np(a.dtype), kind="ExternalInput").ap() for n, a in arrays.items()}
    out = nc.dram_tensor("out", [NODES, D], mybir.dt.float32, kind="ExternalOutput").ap()
    graph_layers(nc, out=out, **args)
    r = run_bass_kernel_spmd(nc, [arrays], core_ids=[0])
    return r.results[0]["out"][:N]
```

```python
import math
from contextlib import ExitStack, contextmanager

import concourse.bass as bass
from concourse import mybir

P = 128
N, E, D = 100000, 25000, 48
R, TYPES, EMB = 40, 119, 32
BATCH = 14
GROUP = 4
PAIRS = BATCH // 2
TILES = 196
CHUNKS = 56
C = 14
HALF = 7
NODES = P * CHUNKS * C
EDGES = TILES * P
DUMP = GROUP * P
ROWS = NODES + DUMP
TRIPS = 7
BATCHES, GROUPS, BLOCKS = 2, TILES // GROUP // TRIPS, TILES // HALF // TRIPS
BUFFERS = 4
BULK_TRIPS = CHUNKS // BUFFERS
SLOTS = CHUNKS // TRIPS
EPS = 1e-5
W = D + 1
DEG, MULT, TYPE, W0 = D, D + 1, D + 2, D + 4
AGG, TOT, W1 = D + 1, 2 * D + 1, 2 * D + 2
W2 = 2 * D + 1

assert C == BATCH
assert TILES == TRIPS * BATCHES * BATCH == TRIPS * GROUPS * GROUP and EDGES >= E
assert NODES >= N + EDGES - E

START, START_DMA = 1, 16
TO_SRC = (0, 1, 1, 0)
PER_FIRST = 4
PER = (57, 20, 42, 22, 0)

def product_stages(of, taker):
    return [("turn " + of, "PE"), ("copy " + of, "ACT"), (of, "PE"), ("take " + of, taker)]


LOOKUP = [("hot", "DVE"), ("turn hot", "PE"), ("copy hot", "ACT"), ("look", "PE")]
NORM = [("square", "ACT"), ("var", "DVE"), ("root", "ACT")]
NORM2 = [("square2", "ACT"), ("var2", "DVE"), ("root2", "ACT")]
PARTS = [("rest", "DVE"), ("part0", "ACT"), ("part1", "ACT")]
EDGE_STAGES = ([("message", "DVE"), *PARTS],
               [("load", "SP"), ("square", "ACT"), *LOOKUP, ("var", "DVE"), ("root", "ACT"), ("norm", "DVE"), ("logit", "DVE"),
                ("message", "DVE"), *PARTS],
               [("rescale", "DVE"), *NORM, ("norm", "DVE"), *product_stages("gamma", "DVE"), *NORM2, ("scale", "DVE"),
                *product_stages("weight", "ACT"), *PARTS],
               [("sum", "DVE"), *NORM, ("scale", "DVE"), *product_stages("weight", "ACT"), *PARTS],
               [])
BULK_STAGES = ([],
               [*NORM, ("norm", "DVE"), ("store", "ACT")],
               [("rescale", "DVE"), *NORM, ("norm", "DVE"), *product_stages("gamma", "DVE"), *NORM2, ("norm2", "DVE"), ("store", "ACT")],
               [("sum", "DVE"), *NORM, ("norm", "DVE"), *product_stages("weight", "DVE"), ("store", "ACT")],
               [("sum", "DVE"), *NORM, ("norm", "DVE"), ("store", "ACT")])
LOOK_STAGES = [*LOOKUP, ("store", "ACT")]
GROUP_STAGES = [("same", "DVE"), ("sums", "PE"), ("stage", "ACT"), ("add", "Pool")]
BASE = {"load": 0, "hot": 2, "turn hot": 2, "copy hot": 2, "look": 2, "square": 2, "var": 2, "root": 1, "norm": 2, "logit": 3,
        "message": 5, "rest": 2, "part0": 1, "part1": 1, "rescale": 4, "turn": 2.5, "copy": 2, "product": 4, "take": 2,
        "square2": 2, "var2": 2, "root2": 1, "scale": 2, "norm2": 2, "store": 1, "sum": 2, "same": 3, "sums": 9, "stage": 3,
        "add": 0, "pull1": 0, "pull0": 0.55, "pull": 0.054, "ahead": 7}
COSTS = ({**BASE, "message": 3, "rest": 1, "trip": 55},
         {**BASE, "root": 4, "logit": 5, "rest": 1, "var2": 3, "pull0": 0.57, "trip": 65},
         {**BASE, "turn hot": 1.5, "copy hot": 2.5, "logit": 4, "sum": 4, "sums": 9.5, "ahead": 6.5, "trip": 86},
         {**BASE, "copy hot": 3, "norm": 3, "part0": 0.5, "copy": 1.5, "scale": 2.5, "norm2": 1, "store": 0.5,
          "same": 5, "sums": 11, "pull1": -0.07, "ahead": 5, "trip": 65},
         {**BASE, "trip": 54})

EDGE_NORMS, BULK_NORMS, EDGE_INPUTS, BULK_INPUTS = (0, 0, 7, 21), (0, 0, 14, 42, 56), (0, 0, 0, 14), (0, 0, 0, 14)


def cost(layer, stage):
    name, _, of = stage.partition(" ")
    return COSTS[layer]["product" if stage in ("gamma", "weight") else name if of in ("gamma", "weight") else stage]


def trip_order(layer):
    c, timed = COSTS[layer], []
    trip = c["trip"]

    def length(stages):
        return sum(cost(layer, name) for name, _ in stages)

    def stream(start, kind, slot, stages):
        for name, engine in stages:
            timed.append((start, len(timed), (kind, slot, name, engine)))
            start += cost(layer, name)

    for v in range(GROUPS if layer < 4 else 0):
        start = (trip - 13) / (GROUPS - 1) * v
        stream(start, "group", v, GROUP_STAGES)
        stream(start - c["ahead"], "group", v, [("load", "SP")])
    for j in range(SLOTS):
        if layer:
            start = (trip - length(BULK_STAGES[layer])) / (SLOTS - 1) * j
            stream(start, "bulk", j, BULK_STAGES[layer])
            stream(start - c["ahead"], "bulk", j, [("load", "SP")])
        if layer < 3:
            stream(trip / SLOTS * j + 2, "start", j, [("load", "SP")])
    for u in range(BATCHES):
        start = (trip - length(EDGE_STAGES[layer])) * u
        stream(start, "edge", u, EDGE_STAGES[layer])
        if layer == 0:
            stream(start + 4, "look", u, LOOK_STAGES)
        for k in range(PAIRS if layer < 4 else 0):
            timed.append((trip * (c["pull%d" % u] + c["pull"] * k), len(timed), ("pull", u, k, "Pool")))
    if layer == 0:
        for v in range(GROUPS):
            start = (trip - 5) / GROUPS * v
            timed += [(start, len(timed), ("count", v, None, "DVE")), (start - c["ahead"], len(timed), ("count", v, None, "SP"))]
        for w in range(BLOCKS):
            timed += [(trip / BLOCKS * w, len(timed), ("gate", w, None, engine)) for engine in ("SP", "PE", "ACT")]
        timed.append((trip, len(timed), ("aim", 0, None, "DVE")))
    return [x for *_, x in sorted(timed, key=lambda y: y[:2])]


ORDERS = [trip_order(layer) for layer in range(5)]
FRESH, LATE = ("edge", "count", "aim", "gate", "look", "start"), ("group", "bulk")
PRODUCTS = [[x[:3] for x in o if x[2] in ("turn gamma", "turn weight")] for o in ORDERS]
for made, o in zip(PRODUCTS, ORDERS):
    for step_ in ("copy ", "", "take "):
        assert [x[:3] for x in o if x[2] in (step_ + "gamma", step_ + "weight")] == \
            [(kind, k, x.replace("turn ", step_)) for kind, k, x in made]


def products_of_trip(layer, t):
    return [x for x in PRODUCTS[layer] if not isinstance(t, int) or x[0] in (LATE if t == TRIPS else FRESH if t == 0 else FRESH + LATE)]


def product_number(layer, t, kind, k, of):
    here = products_of_trip(layer, t)
    before = sum(TRIPS * len(PRODUCTS[a]) for a in range(layer))
    if not (isinstance(t, int) and t == 0):
        before += len(products_of_trip(layer, 0)) + len(PRODUCTS[layer]) * (t - 1)
    return before + here.index((kind, k, "turn " + of))


def slot_of_product(layer, t, kind, k, of):
    return products_of_trip(layer, t).index((kind, k, "turn " + of)) % 2


def graph_layers(nc, x, node_mult, node_type, src_rows, dst_rows, src_tiles, dst_tiles, attr_t, weight_tiles,
                 w1_t, b1, w2_t, b2, emb, emb_t, adapt_t, gamma, beta, weight2, bias2, weight3, bias3, out):
    f32, i32, bf16 = mybir.dt.float32, mybir.dt.int32, mybir.dt.bfloat16
    ALU, ACT, AX = mybir.AluOpType, mybir.ActivationFunctionType, mybir.AxisListType

    def dram(name, shape):
        return nc.dram_tensor(name, shape, f32, kind="Internal").ap()

    rows0 = dram("rows0", [NODES, W0])
    table0, table1, table2 = dram("table0", [ROWS, W0]), dram("table1", [ROWS, W1]), dram("table2", [ROWS, W2])
    base3, agg3 = dram("base3", [NODES, D]), dram("agg3", [ROWS, D])
    gates, src_emb = dram("gates", [P, TILES * D]), dram("src_emb", [P, TILES * EMB])

    def by_chunk(t):
        return t[0:NODES, :].rearrange("(p c) w -> p c w", p=P)

    x_c, rows0_c, table0_c, table1_c, table2_c = by_chunk(x), by_chunk(rows0), by_chunk(table0), by_chunk(table1), by_chunk(table2)
    base3_c, agg3_c, out_c = by_chunk(base3), by_chunk(agg3), by_chunk(out)

    ctx = ExitStack()
    with ctx:
        def sb(name, shape, dt=f32):
            return ctx.enter_context(nc.sbuf_tensor(name, shape, dt))

        def sem(name):
            return ctx.enter_context(nc.semaphore(name))

        def pair(name):
            return [sem(f"{name}_{u}") for u in range(2)]

        def per_buffer(name):
            return [sem(f"{name}_{u}") for u in range(BUFFERS)]

        ident = sb("ident", [P, P])
        ident_b = sb("ident_b", [P, P], bf16)
        earlier = sb("earlier", [P, DUMP + P])
        type_iota = sb("type_iota", [P, TYPES])
        dump_row = sb("dump_row", [P, TILES])
        zeros = sb("zeros", [P, W1])
        eps = sb("eps", [P, 1])
        half_pi = sb("half_pi", [P, 1])
        zero1 = sb("zero1", [P, 1])
        gamma_b = sb("gamma_b", [P, D])
        beta_b = sb("beta_b", [P, D])
        bias2_b = sb("bias2_b", [P, D])
        bias3_b = sb("bias3_b", [P, D])
        w1_sb = sb("w1_sb", [R, D])
        b1_sb = sb("b1_sb", [D, 1])
        w2_sb = sb("w2_sb", [D + 1, D])
        emb_sb = sb("emb_sb", [TYPES, EMB])
        embt_sb = sb("embt_sb", [EMB, TYPES])
        adapt_sb = sb("adapt_sb", [EMB, EMB])
        adapted = sb("adapted", [TYPES, EMB])
        emb_rest = sb("emb_rest", [TYPES, EMB])
        emb_parts = sb("emb_parts", [TYPES, 3, EMB], bf16)
        adapted_parts = sb("adapted_parts", [TYPES, 3, EMB], bf16)
        wide2 = sb("wide2", [2 * D, 2 * D])
        wide3 = sb("wide3", [2 * D, 2 * D])
        wide_gamma = sb("wide_gamma", [2 * D + 1, 2 * D])
        wide_mean = sb("wide_mean", [P, 2])
        src_i = sb("src_i", [P, TILES], i32)
        dst_i = sb("dst_i", [P, TILES], i32)
        src_f = sb("src_f", [P, TILES])
        dst_f = sb("dst_f", [P, TILES])
        ew = sb("ew", [P, TILES])
        cw = sb("cw", [P, TILES])
        src_seen = sb("src_seen", [P, TILES])
        dst_seen = sb("dst_seen", [P, TILES])
        src_to = sb("src_to", [P, TILES], i32)
        dst_to = sb("dst_to", [P, TILES], i32)
        src_type = sb("src_type", [P, TILES])
        dst_deg = sb("dst_deg", [P, TILES])
        parts = sb("parts", [P, TILES, 3, W], bf16)
        rows = sb("rows", [P, 2, BATCH * W1])
        row_index = sb("row_index", [P, 2, BATCH], i32)
        edev = sb("edev", [P, 2, BATCH, D])
        esq = sb("esq", [P, 2, BATCH, D])
        emsg = sb("emsg", [P, 2, BATCH, W])
        erest = sb("erest", [P, 2, BATCH, W])
        evar = sb("evar", [P, 2, BATCH])
        estd = sb("estd", [P, 2, BATCH])
        efac = sb("efac", [P, 2, BATCH])
        efac2 = sb("efac2", [P, 2, BATCH])
        logit = sb("logit", [P, 2, BATCH])
        gate_in = sb("gate_in", [P, 2, BATCH, D])
        emb_in = sb("emb_in", [P, 2, BATCH, EMB])
        onehot = sb("onehot", [P, BATCH, TYPES], bf16)
        hot_turned = sb("hot_turned", [P, BATCH * P], bf16)
        turned = sb("turned", [P, 2, PAIRS * P])
        keyrow = sb("keyrow", [P, 2, DUMP], i32)
        same = sb("same", [P, 2, GROUP, DUMP], bf16)
        to_add = sb("to_add", [P, 2, GROUP * W])
        to_index = sb("to_index", [P, 2, GROUP], i32)
        bin_ = sb("bin", [P, BUFFERS, C * W1])
        bout = sb("bout", [P, BUFFERS, C * W0])
        bdev = sb("bdev", [P, BUFFERS, C, D])
        bsq = sb("bsq", [P, BUFFERS, C, D])
        bvar = sb("bvar", [P, BUFFERS, C])
        bstd = sb("bstd", [P, BUFFERS, C])
        bfac = sb("bfac", [P, BUFFERS, C])
        attr_sb = [bsq[0:R, 2 * u:2 * u + 2, :, :].rearrange("p b c d -> p (b c d)")[:, 0:HALF * P] for u in range(2)]
        hidden = bdev[0:64, 0:2, :, :].rearrange("p b c d -> p (b c d)")[:, 0:HALF * P]
        gate_out = bdev[:, 2, 0:HALF, :]
        looked = bdev[:, 3, :, 0:EMB]
        mult_in, type_in = rows[:, 0, 0:CHUNKS * C], rows[:, 1, 0:CHUNKS * C].bitcast(i32)
        count_keys = bin_[:, :, :].rearrange("p b n -> p (b n)")[:, 0:4 * DUMP].bitcast(i32)\
            .rearrange("p (s k n) -> p s k n", s=2, k=2)
        seen_tmp = edev[:, 0, :, :].rearrange("p b d -> p (b d)")

        ps = ctx.enter_context(nc.psum_tensor("ps", [P, 8, 512], f32))
        flat = ps[:, :, :].rearrange("p b n -> p (b n)")
        ps_turn, ps_prod = [flat[:, 0:1024], flat[:, 3072:4096]], flat[:, 1024:2048]
        ps_hidden = flat[:, 0:1024]
        ps_gate, ps_look = ps[:, 2, :], ps[:, 3, :]
        ps_sum = [ps[:, 4, :], ps[:, 5, :]]
        ps_hot = flat[:, 3072:4096].bitcast(bf16)

        def top_half(t):
            return t.bitcast(bf16).rearrange("p (n h) -> p n h", h=2)[:, :, 1:2].rearrange("p n h -> p (n h)")

        s_const = sem("const_loaded")
        s_built = sem("const_built")
        s_iota = sem("iota_made")
        s_pool = sem("pool_step")
        s_ready = sem("edge_arrays_ready")
        s_centred = sem("weights_centred")
        s_adapt = sem("adapted_product")
        s_adapted = sem("adapted_ready")
        bulk_in, bulk_in2 = per_buffer("bulk_loaded"), per_buffer("bulk_loaded_sum")
        bulk_used, bulk_out, bulk_stored = per_buffer("bulk_used"), per_buffer("bulk_ready"), per_buffer("bulk_stored")
        attr_in = pair("attr_loaded")
        s_hpre, s_hid = sem("hidden_product"), sem("hidden_ready")
        s_gpre, s_gate, s_gstored = sem("gate_product"), sem("gate_ready"), sem("gate_stored")
        s_estored = sem("src_emb_stored")
        s_copied = sem("table0_copied")
        count_in = pair("count_keys_loaded")
        s_zero = [sem(f"sums_started_{k}") for k in range(4)]
        key_in, rows_in, rows_used, index_in = pair("keyrow_loaded"), pair("rows_gathered"), pair("rows_used"), pair("index_staged")
        side_in, side_used = pair("gate_and_emb_loaded"), pair("gate_and_emb_used")
        s_counted = sem("keys_counted")
        s_same, s_summed, s_staged, s_added = sem("same_ready"), sem("sum_product"), sem("sum_staged"), sem("group_added")
        e_dev, e_sqd, e_var, e_std = pair("edge_state"), pair("edge_squared"), pair("edge_variance"), pair("edge_deviation")
        b_dev, b_sqd, b_var, b_std = per_buffer("bulk_state"), per_buffer("bulk_squared"), per_buffer("bulk_variance"), per_buffer("bulk_deviation")
        s_deg, s_degroot = pair("degree_product"), pair("degree_root")
        s_msg, s_rest, s_parts = pair("message_ready"), pair("message_rest"), pair("message_parts")
        s_step = sem("vector_step")
        s_hot, s_hott, s_hotc = sem("onehot_ready"), sem("onehot_turned"), sem("onehot_turned_copied")
        s_look, s_looked = sem("types_looked_up"), sem("lookup_taken")
        e_input, b_input = pair("edge_product_input"), per_buffer("bulk_product_input")
        s_turned, s_turnc = sem("input_turned"), sem("input_turned_copied")
        s_prod, s_taken = sem("product_ready"), sem("product_taken")

        block = ctx.enter_context(nc.Block())

        def apart(engine):
            engine.nop(nofuse=True)

        @block.sync
        def _(sync):
            n = [0]

            def const(to, of):
                sync.dma_start(to, of).then_inc(s_const, 16)
                n[0] += 1

            for started in (*bulk_used, *rows_used, *side_used, *s_parts, s_counted, s_hpre, s_same, s_staged, s_summed,
                            s_hid, s_gate, s_gpre, s_hott, s_hotc, s_look, s_looked, s_taken):
                sync.sem_inc(started, START)
            sync.dma_start(mult_in, node_mult.rearrange("(p c) -> p c", p=P)).then_inc(bulk_stored[0], 16)
            sync.dma_start(type_in, node_type.rearrange("(p c) -> p c", p=P)).then_inc(bulk_stored[1], 16)
            for u in (2, 3):
                sync.dma_start(wide_mean[:, u - 2:u - 1], gamma[0:1].rearrange("(a d) -> a d", a=1).to_broadcast([P, 1]))\
                    .then_inc(bulk_stored[u], 16)
            with sync.Fori(0, BULK_TRIPS) as i:
                for u in range(BUFFERS):
                    sync.wait_ge(bulk_used[u], i + START)
                    sync.dma_start(bin_[:, u, 0:C * D].rearrange("p (c d) -> p c d", d=D),
                                   x_c[:, bass.ds((BUFFERS * i + u) * C, C), :]).then_inc(bulk_in[u], 16)
            sync.wait_ge(s_built, 1)
            const(src_i[:, :], src_tiles)
            const(dst_i[:, :], dst_tiles)
            const(ew[:, :], weight_tiles)
            for to, of in ((gamma_b, gamma), (beta_b, beta), (bias2_b, bias2), (bias3_b, bias3)):
                const(to[:, :], of.rearrange("(a d) -> a d", a=1).to_broadcast([P, D]))
            const(w1_sb[:, :], w1_t)
            const(b1_sb[:, :], b1.rearrange("(d a) -> d a", a=1))
            const(w2_sb[0:D, :], w2_t)
            const(w2_sb[D:D + 1, :], b2.rearrange("(a d) -> a d", a=1))
            const(emb_sb[:, :], emb)
            const(embt_sb[:, :], emb_t)
            const(adapt_sb[:, :], adapt_t)
            for to, of in ((wide2, weight2), (wide3, weight3)):
                for k in range(2):
                    const(to[k * D:k * D + D, k * D:k * D + D], of)
            assert n[0] == 18

            def begin(layer, i, j):
                table, first, of, width = ((table1, AGG, zeros, D + 1), (table2, AGG, bias2_b, D), (agg3, 0, bias3_b, D))[layer]
                sync.dma_start(by_chunk(table)[:, bass.ds((SLOTS * i + j) * C, C), first:first + width],
                               of[:, 0:width].rearrange("p (a w) -> p a w", a=1).to_broadcast([P, C, width]))\
                    .then_inc(s_zero[layer + 1], 16)

            def begin_dump(k, table, width):
                sync.dma_start(table[NODES:ROWS, :].rearrange("(p c) w -> p c w", p=P),
                               zeros[:, 0:width].rearrange("p (a w) -> p a w", a=1).to_broadcast([P, DUMP // P, width]))\
                    .then_inc(s_zero[k], 16)

            def group_keys(layer, i, v):
                g = GROUPS * i + v
                sync.wait_ge(s_same, (GROUPS * TRIPS * layer + (g - 1 if v else g)) + START)
                sync.dma_start(keyrow[:, v % 2, :],
                               (dst_rows, src_rows)[TO_SRC[layer]][:, bass.ds(g * DUMP, DUMP)].to_broadcast([P, DUMP]))\
                    .then_inc(key_in[v % 2], 16)

            sync.wait_ge(s_centred, 1)

            for layer in range(5):
                if layer:
                    sync.wait_ge(s_added, 16 * TILES * layer + START_DMA)
                    for u in range(BUFFERS):
                        sync.wait_ge(bulk_stored[u], 16 * BULK_TRIPS * layer + START_DMA)
                if layer == 1:
                    sync.wait_ge(s_counted, GROUPS * TRIPS + START)
                    sync.wait_ge(s_gstored, 16 * TILES // HALF + START_DMA)
                    sync.wait_ge(s_estored, 16 * TILES // BATCH + START_DMA)

                def trip(i, kinds):
                    for kind, k, stage, engine in ORDERS[layer]:
                        if kind not in kinds or engine != "SP":
                            continue
                        if kind == "group":
                            group_keys(layer, i - 1, k)
                        elif kind == "start":
                            if layer == 0 and isinstance(i, int):
                                n = NODES // SLOTS
                                sync.dma_start(table0[k * n:k * n + n, :], rows0[k * n:k * n + n, :]).then_inc(s_copied, 16)
                            begin(layer, i, k)
                        elif kind == "count":
                            g = GROUPS * i + k
                            sync.wait_ge(s_counted, (g - 1 if k else g) + START)
                            for h in range(2):
                                sync.dma_start(count_keys[:, k % 2, h, :],
                                               (dst_rows, src_rows)[h][:, bass.ds(g * DUMP, DUMP)].to_broadcast([P, DUMP]))\
                                    .then_inc(count_in[k % 2], 16)
                        elif kind == "gate":
                            j = BLOCKS * i + k
                            sync.wait_ge(s_hpre, (j - 1 if k else j) + START)
                            sync.dma_start(attr_sb[k % 2], attr_t[:, bass.ds(j * (HALF * P), HALF * P)]).then_inc(attr_in[k % 2], 16)
                        elif kind == "edge":
                            sync.wait_ge(side_used[k], i + START)
                            at = 2 * i + k
                            sync.dma_start(gate_in[:, k, :, :].rearrange("p t d -> p (t d)"),
                                           gates[:, bass.ds(at * (BATCH * D), BATCH * D)]).then_inc(side_in[k], 16)
                            sync.dma_start(emb_in[:, k, :, :].rearrange("p t d -> p (t d)"),
                                           src_emb[:, bass.ds(at * (BATCH * EMB), BATCH * EMB)]).then_inc(side_in[k], 16)
                        else:
                            u, ii, at = k % BUFFERS, SLOTS // BUFFERS * (i - 1) + k // BUFFERS, bass.ds((SLOTS * (i - 1) + k) * C, C)
                            sync.wait_ge(bulk_used[u], BULK_TRIPS * layer + ii + START)
                            if layer == 4:
                                for h, t in ((0, base3_c), (1, agg3_c)):
                                    sync.dma_start(bin_[:, u, h * C * D:(h + 1) * C * D].rearrange("p (c d) -> p c d", d=D),
                                                   t[:, at, :]).then_inc((bulk_in, bulk_in2)[h][u], 16)
                            else:
                                width = (0, W0, W1, W2)[layer]
                                sync.dma_start(bin_[:, u, 0:C * width].rearrange("p (c w) -> p c w", w=width),
                                               (None, table0_c, table1_c, table2_c)[layer][:, at, :]).then_inc(bulk_in[u], 16)

                if layer == 4:
                    with sync.Fori(1, TRIPS + 1) as i:
                        trip(i, ("bulk",))
                    continue
                if layer == 0:
                    for u in range(BUFFERS):
                        sync.wait_ge(bulk_stored[u], 16 * BULK_TRIPS + START_DMA)
                trip(0, FRESH)
                with sync.Fori(1, TRIPS) as i:
                    trip(i, FRESH + LATE)
                if layer < 3:
                    begin_dump(layer + 1, (table1, table2, agg3)[layer], (W1, W2, D)[layer])
                trip(TRIPS, LATE)

        @block.gpsimd
        def _(pool):
            steps = [0]

            def step(ins):
                steps[0] += 1
                ins.then_inc(s_pool, 1)
                pool.wait_ge(s_pool, steps[0])

            step(pool.memset(wide2[:, :], 0.0))
            step(pool.memset(wide3[:, :], 0.0))
            step(pool.memset(hidden, 1.0))
            step(pool.memset(turned[:, :, :], 1.0))
            pool.memset(zeros[:, :], 0.0).then_inc(s_built, 1)
            pool.wait_ge(s_built, 1)
            pool.dma_start(table0[NODES:ROWS, :].rearrange("(p c) w -> p c w", p=P),
                           zeros[:, 0:W0].rearrange("p (a w) -> p a w", a=1).to_broadcast([P, DUMP // P, W0]))\
                .then_inc(s_added, 16)
            step(pool.memset(ident[:, :], 0.0))
            step(pool.affine_select(out=ident[:, :], in_=ident[:, :], compare_op=ALU.not_equal, fill=1.0,
                                    base=0, pattern=[[-1, P]], channel_multiplier=1))
            step(pool.tensor_copy(ident_b[:, :], ident[:, :]))
            step(pool.memset(earlier[:, :], 1.0))
            step(pool.affine_select(out=earlier[:, :], in_=earlier[:, :], compare_op=ALU.is_gt, fill=0.0,
                                    base=DUMP, pattern=[[-1, DUMP + P]], channel_multiplier=1))
            iota = seen_tmp[:, 0:TYPES].bitcast(i32)
            step(pool.iota(iota, pattern=[[1, TYPES]], base=0, channel_multiplier=0))
            step(pool.tensor_copy(type_iota[:, :], iota))
            iota = seen_tmp[:, TYPES:TYPES + TILES].bitcast(i32)
            step(pool.iota(iota.rearrange("p (g j) -> p g j", j=GROUP), pattern=[[0, TILES // GROUP], [P, GROUP]],
                           base=NODES, channel_multiplier=1))
            pool.tensor_copy(dump_row[:, :], iota).then_inc(s_iota, 1)

            pool.wait_ge(s_const, 16 * 18)

            def pull(layer, i, u, ks):
                table = (rows0, table0, table1, table2)[layer]
                width = (W0, W0, W1, W2)[layer]
                if 0 in ks:
                    key = dst_i if TO_SRC[layer] else src_i
                    pool.wait_ge(rows_used[u], TRIPS * layer + i + START)
                    pool.tensor_copy(row_index[:, u, :], key[:, bass.ds((2 * i + u) * BATCH, BATCH)]).then_inc(index_in[u], 1)
                    pool.wait_ge(index_in[u], TRIPS * layer + i + 1)
                    apart(pool)
                for k in ks:
                    pool.indirect_dma_start(
                        out=rows[:, u, k * width:(k + 1) * width], out_offset=None, in_=table,
                        in_offset=bass.IndirectOffsetOnAxis(ap=row_index[:, u, k:k + 1], axis=0),
                    ).then_inc(rows_in[u], 16)

            def group(layer, i, v):
                to = (table0, table1, table2, agg3)[layer]
                first = (0, AGG, AGG, 0)[layer]
                width = (W, W, D, D)[layer]
                g = GROUPS * TRIPS * layer + GROUPS * i + v
                pool.wait_ge(s_staged, g + 1 + START)
                pool.wait_ge(s_added, 16 * GROUP * g + START_DMA)
                apart(pool)
                for k in range(GROUP):
                    pool.indirect_dma_start(
                        out=to, out_offset=bass.IndirectOffsetOnAxis(ap=to_index[:, v % 2, k:k + 1], axis=0),
                        in_=to_add[:, v % 2, k * width:(k + 1) * width], in_offset=None,
                        element_offset=first, compute_op=ALU.add,
                    ).then_inc(s_added, 16)

            for layer in range(4):
                if layer:
                    pool.wait_ge(s_added, 16 * TILES * layer + START_DMA)
                for u in range(BUFFERS):
                    pool.wait_ge(bulk_stored[u], 16 * BULK_TRIPS * max(layer, 1) + START_DMA)
                pull(layer, 0, 0, range(BATCH))
                pull(layer, 0, 1, range(BATCH))
                pull(layer, 1, 0, range(BATCH))
                if layer:
                    pool.wait_ge(s_zero[layer], 16 * (CHUNKS + 1))
                else:
                    pool.wait_ge(s_copied, 16 * SLOTS)

                def trip(i, last=False):
                    for kind, k, stage, engine in ORDERS[layer]:
                        if engine != "Pool":
                            continue
                        if kind == "group":
                            group(layer, i - 1, k)
                        elif k == 1:
                            pull(layer, i, 1, (2 * stage, 2 * stage + 1))
                        elif not last:
                            pull(layer, i + 1, 0, (2 * stage, 2 * stage + 1))

                with pool.Fori(1, TRIPS - 1) as i:
                    trip(i)
                trip(TRIPS - 1, last=True)
                for v in range(GROUPS):
                    group(layer, TRIPS - 1, v)

        @block.scalar
        def _(act):
            with act.Fori(0, BULK_TRIPS) as i:
                for u in range(BUFFERS):
                    act.wait_ge(bulk_out[u], i + 1)
                    act.dma_start(rows0_c[:, bass.ds((BUFFERS * i + u) * C, C), :],
                                  bout[:, u, :].rearrange("p (c w) -> p c w", w=W0)).then_inc(bulk_stored[u], 16)
            act.wait_ge(s_adapt, 1)
            act.activation(adapted[:, :], ps_gate[0:TYPES, 0:EMB], ACT.Copy).then_inc(s_adapted, 1)
            act.wait_ge(s_const, 16 * 18)

            def group(layer, i, v):
                g = GROUPS * TRIPS * layer + GROUPS * i + v
                width = (W, W, D, D)[layer]
                to = src_to if TO_SRC[layer] else dst_to
                act.wait_ge(s_summed, g + 1 + START)
                act.wait_ge(s_added, 16 * GROUP * (g - 1 if v else g) + START_DMA)
                act.activation(to_index[:, v % 2, :], to[:, bass.ds((GROUPS * i + v) * GROUP, GROUP)], ACT.Copy)
                act.activation(to_add[:, v % 2, 0:GROUP * width], ps_sum[v % 2][:, 0:GROUP * width], ACT.Copy)\
                    .then_inc(s_staged, 1)

            def gate(i, w):
                n = BLOCKS * i + w
                act.wait_ge(s_hpre, n + 1 + START)
                act.wait_ge(s_gpre, n + START)
                act.activation(hidden[0:D, :].rearrange("p (b n) -> p b n", b=2),
                               ps_hidden[0:D, :].rearrange("p (b n) -> p b n", b=2)[:, :, 0:HALF * P // 2],
                               ACT.Silu, bias=b1_sb[:, :]).then_inc(s_hid, 1)
                act.wait_ge(s_gpre, n + 1 + START)
                act.wait_ge(s_gstored, 16 * n + START_DMA)
                act.activation(gate_out, ps_gate[:, 0:HALF * D].rearrange("p (t d) -> p t d", d=D), ACT.Copy).then_inc(s_gate, 1)
                act.wait_ge(s_gate, n + 1 + START)
                act.dma_start(gates[:, bass.ds(n * (HALF * D), HALF * D)], gate_out.rearrange("p t d -> p (t d)"))\
                    .then_inc(s_gstored, 16)

            def square(state, squared, n, dev, sq):
                act.wait_ge(state, n)
                act.activation(sq, dev, ACT.Square).then_inc(squared, 1)

            def root(ready, done, n, var, std):
                act.wait_ge(ready, n + 1)
                act.activation(std, var, ACT.Sqrt, bias=eps[:, :], scale=1.0 / D).then_inc(done, 1)

            def turn_copy(n, slot):
                act.wait_ge(s_turned, n + 1)
                if not isinstance(n, int) or n > 1:
                    act.wait_ge(s_prod, n - 1)
                act.activation(turned[0:2 * D, slot, :], ps_turn[slot][0:2 * D, 0:PAIRS * P], ACT.Copy).then_inc(s_turnc, 1)

            def hot_copy(n):
                act.wait_ge(s_hott, n + 1 + START)
                act.wait_ge(s_look, n + START)
                act.activation(hot_turned[0:TYPES, :], ps_hot[0:TYPES, 0:BATCH * P], ACT.Copy).then_inc(s_hotc, 1)

            def edge(layer, i, u, stage):
                b = 2 * i + u
                n = EDGE_NORMS[layer] + i * (2 if layer == 2 else 1)
                done = TRIPS * layer + i
                tiles = bass.ds(b * BATCH, BATCH)
                dev, sq = edev[:, u, :, :], esq[:, u, :, :]
                if stage == "square" and layer == 1:
                    square(rows_in[u], e_sqd[u], 16 * BATCH * (done + 1),
                           rows[:, u, 0:BATCH * W0].rearrange("p (t w) -> p t w", w=W0)[:, :, 0:D], sq)
                elif stage == "square":
                    square(e_dev[u], e_sqd[u], done - TRIPS * 2 + 1, dev, sq)
                elif stage == "square2":
                    square(s_taken, e_sqd[u], product_number(layer, i, "edge", u, "gamma") + 1 + START, sq, dev)
                elif stage == "copy hot":
                    hot_copy(TILES // BATCH + b)
                elif stage in ("root", "root2"):
                    root(e_var[u], e_std[u], n + (stage == "root2"), evar[:, u, :], estd[:, u, :])
                    if layer == 3:
                        act.wait_ge(s_deg[u], i + 1)
                        act.activation(efac[:, u, :], efac[:, u, :], ACT.Sqrt, bias=zero1[:, :]).then_inc(s_degroot[u], 1)
                elif stage in ("copy gamma", "copy weight"):
                    turn_copy(product_number(layer, i, "edge", u, stage[5:]), slot_of_product(layer, i, "edge", u, stage[5:]))
                elif stage == "take weight":
                    act.wait_ge(s_prod, product_number(layer, i, "edge", u, "weight") + 1)
                    act.wait_ge(s_parts[u], 2 * done + START)
                    act.activation(emsg[:, u, :, 0:D].rearrange("p (q k) d -> p q k d", k=2),
                                   ps_prod[:, 0:PAIRS * P].rearrange("p (q n) -> p q n", n=P)[:, :, 0:2 * D]
                                   .rearrange("p q (k d) -> p q k d", k=2), ACT.Copy).then_inc(s_taken, 1)
                elif stage in ("part0", "part1"):
                    k = int(stage[4])
                    if layer < 2 or k:
                        act.wait_ge((s_msg, s_rest)[k][u], done + 1)
                    else:
                        act.wait_ge(s_taken, product_number(layer, i, "edge", u, "weight") + 1 + START)
                    act.activation(parts[:, tiles, k, :], top_half((emsg, erest)[k][:, u, :, :].rearrange("p t w -> p (t w)"))
                                   .rearrange("p (t w) -> p t w", w=W), ACT.Copy).then_inc(s_parts[u], 1)

            def bulk(layer, i, j, stage):
                u, ii = j % BUFFERS, SLOTS // BUFFERS * i + j // BUFFERS
                n = BULK_NORMS[layer] + ii * (2 if layer == 2 else 1)
                dev, sq = bdev[:, u, :, :], bsq[:, u, :, :]
                if stage == "square" and layer == 1:
                    square(bulk_in[u], b_sqd[u], 16 * (BULK_TRIPS * layer + ii + 1),
                           bin_[:, u, 0:C * W0].rearrange("p (c w) -> p c w", w=W0)[:, :, 0:D], sq)
                elif stage == "square":
                    square(b_dev[u], b_sqd[u], n - BULK_NORMS[2] + 1, dev, sq)
                elif stage == "square2":
                    square(b_dev[u], b_sqd[u], n - BULK_NORMS[2] + 2, sq, dev)
                elif stage in ("root", "root2"):
                    root(b_var[u], b_std[u], n + (stage == "root2"), bvar[:, u, :], bstd[:, u, :])
                elif stage in ("copy gamma", "copy weight"):
                    turn_copy(product_number(layer, i + 1, "bulk", j, stage[5:]), slot_of_product(layer, i + 1, "bulk", j, stage[5:]))
                elif stage == "store":
                    width = (0, D + 1, D + 1, D, D)[layer]
                    act.wait_ge(bulk_out[u], BULK_TRIPS * layer + ii + 1)
                    act.dma_start((None, table1_c, table2_c, base3_c, out_c)[layer][:, bass.ds((SLOTS * i + j) * C, C), 0:width],
                                  bout[:, u, 0:C * width].rearrange("p (c w) -> p c w", w=width)).then_inc(bulk_stored[u], 16)

            act.wait_ge(s_built, 1)
            act.dma_start(gates[:, 0:D], zeros[:, 0:D]).then_inc(s_gstored, 16)
            act.dma_start(src_emb[:, 0:EMB], zeros[:, 0:EMB]).then_inc(s_estored, 16)

            def look(i, u, stage):
                n = 2 * i + u
                if stage == "copy hot":
                    hot_copy(n)
                else:
                    act.wait_ge(s_look, n + 1 + START)
                    act.wait_ge(s_estored, 16 * n + START_DMA)
                    act.activation(looked, ps_look[:, 0:BATCH * EMB].rearrange("p (t d) -> p t d", d=EMB), ACT.Copy)\
                        .then_inc(s_looked, 1)
                    act.wait_ge(s_looked, n + 1 + START)
                    act.dma_start(src_emb[:, bass.ds(n * (BATCH * EMB), BATCH * EMB)].rearrange("p (t d) -> p t d", d=EMB),
                                  looked).then_inc(s_estored, 16)

            def trip(layer, i, kinds):
                for kind, k, stage, engine in ORDERS[layer]:
                    if kind not in kinds or engine != "ACT":
                        continue
                    if kind == "group":
                        group(layer, i - 1, k)
                    elif kind == "edge":
                        edge(layer, i, k, stage)
                    elif kind == "bulk":
                        bulk(layer, i - 1, k, stage)
                    elif kind == "gate":
                        gate(i, k)
                    else:
                        look(i, k, stage)

            for layer in range(4):
                trip(layer, 0, FRESH)
                with act.Fori(1, TRIPS) as i:
                    trip(layer, i, FRESH + LATE)
                trip(layer, TRIPS, LATE)
                if layer == 0:
                    act.wait_ge(s_ready, 1)
                    act.activation(cw[:, :], cw[:, :], ACT.Sin, bias=half_pi[:, :], scale=-math.pi / 12).then_inc(s_ready, 1)
                    act.wait_ge(s_ready, 2)
                    act.activation(cw[:, :], cw[:, :], ACT.Square).then_inc(s_ready, 1)
            with act.Fori(1, TRIPS + 1) as i:
                trip(4, i, ("bulk",))
            for u in range(BUFFERS):
                act.wait_ge(bulk_stored[u], 16 * BULK_TRIPS * 5 + START_DMA)

        @block.tensor
        def _(pe):
            pe.wait_ge(s_const, 16 * 18)
            pe.wait_ge(s_iota, 1)
            pe.matmul(ps_gate[0:TYPES, 0:EMB], lhsT=embt_sb[:, :], rhs=adapt_sb[:, :], start=True, stop=True)\
                .then_inc(s_adapt, 1)
            pe.wait_ge(s_adapted, 1)

            def gate(i, w):
                n = BLOCKS * i + w
                pe.wait_ge(attr_in[w % 2], 16 * (BLOCKS // 2 * i + w // 2 + 1))
                pe.wait_ge(s_hid, n + START)
                apart(pe)
                for k in range(2):
                    last = pe.matmul(ps_hidden[0:D, k * 512:k * 512 + HALF * P // 2], lhsT=w1_sb[:, :],
                                     rhs=attr_sb[w % 2][:, k * HALF * P // 2:(k + 1) * HALF * P // 2], start=True, stop=True)
                last.then_inc(s_hpre, 1)
                pe.wait_ge(s_hid, n + 1 + START)
                pe.wait_ge(s_gate, n + START)
                for k in range(HALF):
                    last = pe.matmul(ps_gate[:, k * D:(k + 1) * D], lhsT=hidden[0:D + 1, k * P:(k + 1) * P],
                                     rhs=w2_sb[:, :], start=True, stop=True)
                last.then_inc(s_gpre, 1)

            def group(layer, i, v):
                g = GROUPS * TRIPS * layer + GROUPS * i + v
                width = (W, W, D, D)[layer]
                for u in range(2):
                    if v == u * BATCH // GROUP:
                        pe.wait_ge(s_parts[u], 2 * (TRIPS * layer + i + 1) + START)
                pe.wait_ge(s_same, g + 1 + START)
                pe.wait_ge(s_staged, (g - 1 if v else g) + START)
                for to in range(GROUP):
                    for of in range(GROUP):
                        for k in range(3):
                            last = pe.matmul(ps_sum[v % 2][:, to * width:(to + 1) * width],
                                             lhsT=same[:, v % 2, of, to * P:(to + 1) * P],
                                             rhs=parts[:, bass.ds((GROUPS * i + v) * GROUP + of, 1), k, 0:width]
                                             .rearrange("p a w -> p (a w)"),
                                             start=(of == k == 0), stop=(of == GROUP - 1 and k == 2))
                last.then_inc(s_summed, 1)

            def turn_hot(n):
                pe.wait_ge(s_hot, n + 1)
                pe.wait_ge(s_hotc, n + START)
                for t in range(BATCH):
                    last = pe.transpose(ps_hot[0:TYPES, t * P:(t + 1) * P], onehot[:, t, :], ident_b[:, :])
                last.then_inc(s_hott, 1)

            def look(n, table):
                pe.wait_ge(s_hotc, n + 1 + START)
                pe.wait_ge(s_looked, n + START)
                for t in range(BATCH):
                    for k in range(3):
                        last = pe.matmul(ps_look[:, t * EMB:(t + 1) * EMB], lhsT=hot_turned[0:TYPES, t * P:(t + 1) * P],
                                         rhs=table[:, k, :], start=(k == 0), stop=(k == 2))
                last.then_inc(s_look, 1)

            def turn(n, slot, of):
                if not isinstance(n, int) or n > 1:
                    pe.wait_ge(s_turnc, n - 1)
                for q in range(PAIRS):
                    last = pe.transpose(ps_turn[slot][0:2 * D, q * P:(q + 1) * P], of[:, q * 2 * D:(q + 1) * 2 * D], ident[:, :])
                last.then_inc(s_turned, 1)

            def product(n, slot, weights, rows_):
                pe.wait_ge(s_turnc, n + 1)
                pe.wait_ge(s_taken, n + START)
                for q in range(PAIRS):
                    last = pe.matmul(ps_prod[:, q * P:q * P + 2 * D], lhsT=turned[0:rows_, slot, q * P:(q + 1) * P],
                                     rhs=weights[:, :], start=True, stop=True)
                last.then_inc(s_prod, 1)

            def trip(layer, i, kinds):
                for kind, k, stage, engine in ORDERS[layer]:
                    if kind not in kinds or engine != "PE":
                        continue
                    if kind == "group":
                        group(layer, i - 1, k)
                    elif kind == "gate":
                        gate(i, k)
                    elif stage == "turn hot":
                        turn_hot(TILES // BATCH * layer + 2 * i + k)
                    elif stage == "look":
                        look(TILES // BATCH * layer + 2 * i + k, (emb_parts, adapted_parts)[layer])
                    else:
                        of = stage.split()[-1]
                        n, slot = product_number(layer, i, kind, k, of), slot_of_product(layer, i, kind, k, of)
                        if stage == of:
                            if of == "gamma":
                                product(n, slot, wide_gamma, 2 * D + 1)
                            else:
                                product(n, slot, (wide2, wide3)[layer - 2], 2 * D)
                        elif kind == "edge":
                            pe.wait_ge(e_input[k], EDGE_INPUTS[layer] + (2 * i + (of == "weight") if layer == 2 else i) + 1)
                            turn(n, slot, edev[:, k, :, :].rearrange("p t d -> p (t d)"))
                        else:
                            u = k % BUFFERS
                            pe.wait_ge(b_input[u], BULK_INPUTS[layer] + SLOTS // BUFFERS * (i - 1) + k // BUFFERS + 1)
                            turn(n, slot, bdev[:, u, :, :].rearrange("p c d -> p (c d)"))

            for layer in range(4):
                trip(layer, 0, FRESH)
                with pe.Fori(1, TRIPS) as i:
                    trip(layer, i, FRESH + LATE)
                trip(layer, TRIPS, LATE)

        @block.vector
        def _(dve):
            class Steps:
                base, k, i, per = 0, 0, None, 0

                def __call__(self, ins):
                    ins.then_inc(s_step, 1)
                    self.k += 1
                    done = self.base + self.k
                    dve.wait_ge(s_step, done if self.i is None else self.i * self.per + done)

            step = Steps()

            @contextmanager
            def loop(first, end, per):
                with dve.Fori(first, end) as i:
                    step.base, step.k, step.i, step.per = step.base + step.k - first * per, 0, i, per
                    yield i
                    assert step.k == per, step.k
                step.base, step.k, step.i = step.base + end * per, 0, None

            def over(stat, k):
                return stat.rearrange("p (t a) -> p t a", a=1).to_broadcast([P, k, D])

            def column(row, k):
                return row[:, :, k:k + 1].rearrange("p t a -> p (t a)")

            def pairs(prod):
                return prod[:, 0:PAIRS * P].rearrange("p (q n) -> p q n", n=P)[:, :, 0:2 * D].rearrange("p q (k d) -> p q k d", k=2)

            def by_pair(t):
                return t.rearrange("p (q k) d -> p q k d", k=2)

            dve.memset(eps[:, :], EPS)
            dve.memset(half_pi[:, :], math.pi / 2)
            dve.memset(emsg[:, :, :, D:W], 1.0)
            step(dve.memset(zero1[:, :], 0.0))
            step(dve.memset(bout[:, :, :], 0.0))
            for u in range(BUFFERS):
                dve.wait_ge(bulk_stored[u], START_DMA)
            mult_c = mult_in.rearrange("p (c a) -> p c a", a=1)
            type_c = type_in.rearrange("p (c a) -> p c a", a=1)
            with loop(0, BULK_TRIPS, PER_FIRST) as i:
                for u in range(BUFFERS):
                    o = bout[:, u, :].rearrange("p (c w) -> p c w", w=W0)
                    of = bin_[:, u, 0:C * D].rearrange("p (c d) -> p c d", d=D)
                    at = bass.ds((BUFFERS * i + u) * C, C)
                    dve.wait_ge(bulk_in[u], 16 * i + 16)
                    step(dve.reduce_sum(bvar[:, u, :], of, AX.X))
                    dve.wait_ge(bulk_stored[u], 16 * i + START_DMA)
                    dve.scalar_tensor_tensor(o[:, :, 0:D], over(bvar[:, u, :], C), -1.0 / D, of, ALU.mult, ALU.add)\
                        .then_inc(bulk_used[u], 1)
                    dve.tensor_copy(o[:, :, MULT:MULT + 1], mult_c[:, at, :])
                    dve.tensor_copy(o[:, :, TYPE:TYPE + 1], type_c[:, at, :]).then_inc(bulk_out[u], 1)
            dve.wait_ge(s_const, 16 * 18)
            dve.wait_ge(s_iota, 1)
            step(dve.tensor_copy(src_f[:, :], src_i[:, :]))
            step(dve.tensor_copy(dst_f[:, :], dst_i[:, :]))
            dve.tensor_scalar(cw[:, :], ew[:, :], 6.0, None, ALU.min).then_inc(s_ready, 1)
            step(dve.tensor_tensor(wide_gamma[0:2 * D, :].rearrange("p (k d) -> p k d", k=2),
                                   ident[0:2 * D, 0:2 * D].rearrange("p (k d) -> p k d", k=2),
                                   gamma_b[0:2 * D, :].rearrange("p (k d) -> p k d", k=1).to_broadcast([2 * D, 2, D]), ALU.mult))
            step(dve.tensor_copy(wide_gamma[2 * D:2 * D + 1, :].rearrange("p (k d) -> p k d", k=2),
                                 beta_b[2 * D:2 * D + 1, :].rearrange("p (k d) -> p k d", k=1).to_broadcast([1, 2, D])))
            for t, k in ((wide_gamma, 2), (wide2, 2), (wide3, 2), (bias2_b, 1), (bias3_b, 1)):
                blocks = t[:, :].rearrange("p (k d) -> p k d", k=k)
                p = t.shape[0]
                mean = wide_mean[0:p, 0:k]
                step(dve.reduce_sum(mean, blocks, AX.X))
                ins = dve.scalar_tensor_tensor(blocks, mean.rearrange("p (k a) -> p k a", a=1).to_broadcast([p, k, D]),
                                               -1.0 / D, blocks, ALU.mult, ALU.add)
                if t is bias3_b:
                    ins.then_inc(s_centred, 1)
                else:
                    step(ins)
            dve.wait_ge(s_adapted, 1)
            for t, to in ((emb_sb, emb_parts), (adapted, adapted_parts)):
                step(dve.tensor_copy(to[:, 0, :], top_half(t[:, :])))
                step(dve.tensor_tensor(emb_rest[:, :], t[:, :], to[:, 0, :], ALU.subtract))
                step(dve.tensor_copy(to[:, 1, :], top_half(emb_rest[:, :])))
                step(dve.tensor_tensor(to[:, 2, :], emb_rest[:, :], to[:, 1, :], ALU.subtract))

            same_key = (dst_f, src_f, src_f, dst_f)

            def count(i, v):
                g = GROUPS * i + v
                per = 4 if v % 2 == 0 else 3
                dve.wait_ge(count_in[v % 2], i * (per * 32) + (v // 2 + 1) * 32)
                for k, (key, seen) in enumerate(((dst_f, dst_seen), (src_f, src_seen))):
                    for j in range(GROUP):
                        at = bass.ds(g * GROUP + j, 1)
                        last = dve.scalar_tensor_tensor(
                            seen_tmp[:, 0:(j + 1) * P], count_keys[:, v % 2, k, 0:(j + 1) * P], key[:, at],
                            earlier[:, DUMP - j * P:DUMP + P], ALU.is_equal, ALU.mult, accum_out=seen[:, at])
                        if k == 0 or j < GROUP - 1:
                            step(last)
                last.then_inc(s_counted, 1)
                dve.wait_ge(s_counted, g + 1 + START)

            def group(layer, i, v):
                g = GROUPS * TRIPS * layer + GROUPS * i + v
                per = 4 if v % 2 == 0 else 3
                before = TRIPS * per * 16 * layer
                dve.wait_ge(key_in[v % 2], before + i * (per * 16) + (v // 2 + 1) * 16)
                dve.wait_ge(s_summed, (g - 1 if v else g) + START)
                for j in range(GROUP):
                    last = dve.tensor_scalar(same[:, v % 2, j, :], keyrow[:, v % 2, :],
                                             same_key[layer][:, bass.ds((GROUPS * i + v) * GROUP + j, 1)], None, ALU.is_equal)
                last.then_inc(s_same, 1)

            def hot(n, types):
                dve.wait_ge(s_hott, n + START)
                dve.tensor_tensor(onehot[:, :, :],
                                  type_iota[:, :].rearrange("p (a n) -> p a n", a=1).to_broadcast([P, BATCH, TYPES]),
                                  types.to_broadcast([P, BATCH, TYPES]), ALU.is_equal).then_inc(s_hot, 1)

            def variance(squared, n, sq, var, ready):
                dve.wait_ge(squared, n + 1)
                dve.reduce_sum(var, sq, AX.X).then_inc(ready, 1)

            def inverse(std, done, n, free=None):
                dve.wait_ge(done, n + 1)
                ins = dve.reciprocal(std, std)
                if free:
                    ins.then_inc(free[0], 1)
                    dve.wait_ge(*free)
                else:
                    step(ins)

            def rescale(row, dev, fac, k, ready):
                step(dve.tensor_scalar(fac, column(row, TOT), 1e-8, None, ALU.max))
                step(dve.reciprocal(fac, fac))
                step(dve.tensor_tensor(dev, row[:, :, AGG:AGG + D], over(fac, k), ALU.mult))
                dve.tensor_tensor(dev, dev, row[:, :, 0:D], ALU.add).then_inc(ready, 1)

            def edge(layer, i, u, stage):
                b = 2 * i + u
                width = (W0, W0, W1, W2)[layer]
                row = rows[:, u, 0:BATCH * width].rearrange("p (t w) -> p t w", w=width)
                tiles = bass.ds(b * BATCH, BATCH)
                n = EDGE_NORMS[layer] + i * (2 if layer == 2 else 1)
                done = TRIPS * layer + i
                dev, sq, msg, rest = edev[:, u, :, :], esq[:, u, :, :], emsg[:, u, :, :], erest[:, u, :, :]
                var, std, fac, fac2 = evar[:, u, :], estd[:, u, :], efac[:, u, :], efac2[:, u, :]
                if stage == next(name for name, engine in EDGE_STAGES[layer] if engine == "DVE"):
                    dve.wait_ge(rows_in[u], 16 * BATCH * (done + 1))
                if stage == "rest":
                    flat_msg, flat_rest = (t.rearrange("p t w -> p (t w)") for t in (msg, rest))
                    if layer < 2:
                        dve.wait_ge(s_msg[u], done + 1)
                    else:
                        dve.wait_ge(s_taken, product_number(layer, i, "edge", u, "weight") + 1 + START)
                        dve.wait_ge(s_parts[u], 2 * done + START)
                    dve.tensor_tensor(flat_rest, flat_msg, top_half(flat_msg), ALU.subtract).then_inc(s_rest[u], 1)
                    dve.wait_ge(s_rest[u], done + 1)
                    dve.tensor_tensor(parts[:, tiles, 2, :], rest, top_half(flat_rest).rearrange("p (t w) -> p t w", w=W),
                                      ALU.subtract)
                elif layer == 0:
                    dve.wait_ge(s_parts[u], 2 * done + START)
                    dve.tensor_tensor(msg[:, :, 0:D], row[:, :, 0:D], over(ew[:, tiles], BATCH), ALU.mult).then_inc(s_msg[u], 1)
                    dve.tensor_copy(src_type[:, tiles], column(row, TYPE)).then_inc(rows_used[u], 1)
                elif stage == "hot":
                    hot(TILES // BATCH + b, row[:, :, TYPE:TYPE + 1])
                elif stage == "rescale":
                    rescale(row, dev, fac, BATCH, e_dev[u])
                elif stage == "sum":
                    dve.tensor_tensor(dev, row[:, :, 0:D], row[:, :, AGG:AGG + D], ALU.add).then_inc(e_dev[u], 1)
                    step(dve.tensor_scalar(fac2, dst_deg[:, tiles], 1.0, None, ALU.add))
                    dve.scalar_tensor_tensor(fac, column(row, DEG), 1.0, fac2, ALU.add, ALU.mult).then_inc(s_deg[u], 1)
                elif stage in ("var", "var2"):
                    variance(e_sqd[u], n + (stage == "var2"), dev if stage == "var2" else sq, var, e_var[u])
                elif stage == "norm":
                    inverse(std, e_std[u], n)
                    ins = dve.tensor_tensor(dev, dev if layer == 2 else row[:, :, 0:D], over(std, BATCH), ALU.mult)
                    if layer == 2:
                        ins.then_inc(e_input[u], 1)
                    else:
                        step(ins)
                elif stage == "take gamma":
                    m = product_number(layer, i, "edge", u, "gamma")
                    dve.wait_ge(s_prod, m + 1)
                    dve.tensor_tensor(by_pair(sq), pairs(ps_prod), by_pair(row[:, :, 0:D]), ALU.add).then_inc(s_taken, 1)
                elif stage == "scale":
                    if layer == 2:
                        inverse(std, e_std[u], n + 1, (rows_used[u], done + 1 + START))
                        step(dve.tensor_tensor(fac, std, ew[:, tiles], ALU.mult))
                        dve.tensor_tensor(dev, sq, over(fac, BATCH), ALU.mult).then_inc(e_input[u], 1)
                    else:
                        dve.wait_ge(s_degroot[u], i + 1)
                        step(dve.reciprocal(fac, fac))
                        inverse(std, e_std[u], n, (rows_used[u], done + 1 + START))
                        step(dve.tensor_tensor(fac, fac, std, ALU.mult))
                        dve.tensor_tensor(dev, dev, over(fac, BATCH), ALU.mult).then_inc(e_input[u], 1)
                elif stage == "logit":
                    dve.wait_ge(s_look, TILES // BATCH + b + 1 + START)
                    dve.wait_ge(side_in[u], 32 * (i + 1))
                    dve.tensor_tensor(emb_in[:, u, :, :], ps_look[:, 0:BATCH * EMB].rearrange("p (t d) -> p t d", d=EMB),
                                      emb_in[:, u, :, :], ALU.mult).then_inc(s_looked, 1)
                    dve.wait_ge(s_looked, TILES // BATCH + b + 1 + START)
                    step(dve.reduce_sum(logit[:, u, :], emb_in[:, u, :, :], AX.X))
                elif stage == "message" and layer == 1:
                    gate = gate_in[:, u, :, :]
                    dve.tensor_copy(dst_deg[:, tiles], column(row, DEG))
                    dve.wait_ge(s_parts[u], 2 * done + START)
                    dve.tensor_copy(msg[:, :, D:W], row[:, :, MULT:MULT + 1])
                    dve.tensor_tensor(fac, cw[:, tiles], column(row, MULT), ALU.mult).then_inc(rows_used[u], 1)
                    step(dve.tensor_tensor(gate, gate, over(logit[:, u, :], BATCH), ALU.add))
                    step(dve.tensor_tensor(gate, gate, dev, ALU.mult))
                    dve.wait_ge(rows_used[u], done + 1 + START)
                    dve.tensor_tensor(dev, gate, over(fac, BATCH), ALU.mult).then_inc(side_used[u], 1)
                    dve.wait_ge(side_used[u], i + 1 + START)
                    step(dve.reduce_sum(fac2, dev, AX.X))
                    dve.scalar_tensor_tensor(msg[:, :, 0:D], over(fac2, BATCH), -1.0 / D, dev, ALU.mult, ALU.add)\
                        .then_inc(s_msg[u], 1)

            def bulk(layer, i, j, stage):
                u, ii = j % BUFFERS, SLOTS // BUFFERS * i + j // BUFFERS
                width = (0, W0, W1, W2, D)[layer]
                row = bin_[:, u, 0:C * width].rearrange("p (c w) -> p c w", w=width)
                wo = (0, D + 1, D + 1, D, D)[layer]
                o = bout[:, u, 0:C * wo].rearrange("p (c w) -> p c w", w=wo)
                n = BULK_NORMS[layer] + ii * (2 if layer == 2 else 1)
                done = BULK_TRIPS * layer + ii
                dev, sq, var, std, fac = bdev[:, u, :, :], bsq[:, u, :, :], bvar[:, u, :], bstd[:, u, :], bfac[:, u, :]
                free = (bulk_used[u], done + 1 + START)
                if stage in ("rescale", "sum"):
                    dve.wait_ge(bulk_in[u], 16 * (done + 1))
                    if layer == 2:
                        rescale(row, dev, fac, C, b_dev[u])
                    elif layer == 3:
                        step(dve.tensor_scalar(fac, column(row, DEG), 1.0, None, ALU.add))
                        step(dve.reciprocal(fac, fac))
                        dve.tensor_tensor(dev, row[:, :, 0:D], row[:, :, AGG:AGG + D], ALU.add).then_inc(b_dev[u], 1)
                    else:
                        dve.wait_ge(bulk_in2[u], 16 * (ii + 1))
                        dve.wait_ge(bulk_out[u], done)
                        sums = bin_[:, u, C * D:2 * C * D].rearrange("p (c d) -> p c d", d=D)
                        dve.tensor_tensor(dev, row, sums, ALU.add).then_inc(b_dev[u], 1)
                elif stage in ("var", "var2"):
                    variance(b_sqd[u], n + (stage == "var2"), dev if stage == "var2" else sq, var, b_var[u])
                elif stage == "norm":
                    if layer in (1, 4):
                        dve.wait_ge(bulk_stored[u], 16 * done + START_DMA)
                    if layer == 1:
                        dve.tensor_copy(o[:, :, D:D + 1], row[:, :, DEG:DEG + 1])
                        inverse(std, b_std[u], n)
                        dve.tensor_tensor(o[:, :, 0:D], row[:, :, 0:D], over(std, C), ALU.mult).then_inc(bulk_out[u], 1)
                        dve.wait_ge(bulk_out[u], done + 1)
                        dve.tensor_copy(fac, std).then_inc(bulk_used[u], 1)
                    elif layer == 2:
                        inverse(std, b_std[u], n)
                        dve.tensor_tensor(dev, dev, over(std, C), ALU.mult).then_inc(b_input[u], 1)
                    else:
                        inverse(std, b_std[u], n, free)
                        to, signal = (dev, b_input[u]) if layer == 3 else (o, bulk_out[u])
                        dve.tensor_tensor(to, dev, over(std, C), ALU.mult).then_inc(signal, 1)
                elif stage == "take gamma":
                    m = product_number(layer, i + 1, "bulk", j, "gamma")
                    dve.wait_ge(s_prod, m + 1)
                    dve.tensor_tensor(by_pair(sq), pairs(ps_prod), by_pair(row[:, :, 0:D]), ALU.add).then_inc(s_taken, 1)
                    dve.wait_ge(bulk_stored[u], 16 * done + START_DMA)
                    dve.wait_ge(s_taken, m + 1 + START)
                    dve.tensor_copy(o[:, :, D:D + 1], row[:, :, DEG:DEG + 1]).then_inc(b_dev[u], 1)
                elif stage == "norm2":
                    inverse(std, b_std[u], n + 1, free)
                    dve.tensor_tensor(o[:, :, 0:D], sq, over(std, C), ALU.mult).then_inc(bulk_out[u], 1)
                elif stage == "take weight":
                    m = product_number(layer, i + 1, "bulk", j, "weight")
                    dve.wait_ge(bulk_stored[u], 16 * done + START_DMA)
                    dve.wait_ge(s_prod, m + 1)
                    scale = fac.rearrange("p (q k a) -> p q k a", k=2, a=1).to_broadcast([P, PAIRS, 2, D])
                    dve.tensor_tensor(by_pair(o), pairs(ps_prod), scale, ALU.mult).then_inc(s_taken, 1)
                    dve.wait_ge(s_taken, m + 1 + START)
                    dve.tensor_tensor(o, o, dev, ALU.add).then_inc(bulk_out[u], 1)

            def aim(i):
                at = bass.ds(i * (GROUPS * GROUP), GROUPS * GROUP)
                for key, seen, to in ((dst_f, dst_seen, dst_to), (src_f, src_seen, src_to)):
                    tmp = seen_tmp[:, 0:GROUPS * GROUP]
                    step(dve.tensor_scalar(seen[:, at], seen[:, at], 1.0, None, ALU.min))
                    step(dve.tensor_tensor(tmp, dump_row[:, at], key[:, at], ALU.subtract))
                    step(dve.tensor_tensor(tmp, tmp, seen[:, at], ALU.mult))
                    step(dve.tensor_tensor(to[:, at], key[:, at], tmp, ALU.add))

            def trip(layer, i, kinds):
                for kind, k, stage, engine in ORDERS[layer]:
                    if kind not in kinds or engine != "DVE":
                        continue
                    if kind == "group":
                        group(layer, i - 1, k)
                    elif kind == "edge":
                        edge(layer, i, k, stage)
                    elif kind == "bulk":
                        bulk(layer, i - 1, k, stage)
                    elif kind == "count":
                        count(i, k)
                    elif kind == "aim":
                        aim(i)
                    else:
                        dve.wait_ge(rows_used[k], i + 1 + START)
                        hot(2 * i + k, src_type[:, bass.ds((2 * i + k) * BATCH, BATCH)].rearrange("p (t a) -> p t a", a=1))

            for layer in range(4):
                if layer == 1:
                    dve.wait_ge(s_gate, TILES // HALF + START)
                    dve.wait_ge(s_ready, 3)
                trip(layer, 0, FRESH)
                with loop(1, TRIPS, PER[layer]) as i:
                    trip(layer, i, FRESH + LATE)
                trip(layer, TRIPS, LATE)
            with loop(1, TRIPS + 1, PER[4]) as i:
                trip(4, i, ("bulk",))


_PADDED = EDGES - E


def kernel(x, src, dst, edge_attr_40, edge_weight, node_type_119, node_vec, L1_gnn_W1, L1_gnn_b1, L1_gnn_W2,
           L1_gnn_b2, L1_gnn_emb, L1_gnn_adaptW, L1_gnn_gamma, L1_gnn_beta, L2_gnn_weight, L2_gnn_bias,
           L3_gnn_W, L3_gnn_b):
    import numpy as np
    import concourse.bacc as bacc
    from concourse.bass_utils import run_bass_kernel_spmd

    def padded(a, n):
        out = np.zeros((n, *a.shape[1:]), a.dtype)
        out[:len(a)] = a
        return out

    def edge_keys(a):
        return np.concatenate([a, np.arange(N, N + _PADDED, dtype=a.dtype)])

    def tiles(a):
        return np.ascontiguousarray(a.reshape(TILES, P).T)

    t = np.ascontiguousarray
    src, dst = edge_keys(np.asarray(src)), edge_keys(np.asarray(dst))
    arrays = {
        "x": padded(np.asarray(x), NODES), "node_mult": padded(np.asarray(node_vec), NODES),
        "node_type": padded(np.asarray(node_type_119), NODES),
        "src_rows": src.reshape(1, EDGES), "dst_rows": dst.reshape(1, EDGES),
        "src_tiles": tiles(src), "dst_tiles": tiles(dst),
        "attr_t": t(padded(np.asarray(edge_attr_40), EDGES).T), "weight_tiles": tiles(padded(np.asarray(edge_weight), EDGES)),
        "w1_t": t(np.asarray(L1_gnn_W1).T), "b1": np.asarray(L1_gnn_b1), "w2_t": t(np.asarray(L1_gnn_W2).T),
        "b2": np.asarray(L1_gnn_b2), "emb": np.asarray(L1_gnn_emb), "emb_t": t(np.asarray(L1_gnn_emb).T),
        "adapt_t": t(np.asarray(L1_gnn_adaptW).T), "gamma": np.asarray(L1_gnn_gamma), "beta": np.asarray(L1_gnn_beta),
        "weight2": np.asarray(L2_gnn_weight), "bias2": np.asarray(L2_gnn_bias),
        "weight3": np.asarray(L3_gnn_W), "bias3": np.asarray(L3_gnn_b),
    }
    nc = bacc.Bacc("TRN2", target_bir_lowering=False, num_devices=1)
    args = {n: nc.dram_tensor(n, a.shape, mybir.dt.from_np(a.dtype), kind="ExternalInput").ap() for n, a in arrays.items()}
    out = nc.dram_tensor("out", [NODES, D], mybir.dt.float32, kind="ExternalOutput").ap()
    graph_layers(nc, out=out, **args)
    r = run_bass_kernel_spmd(nc, [arrays], core_ids=[0])
    return r.results[0]["out"][:N]
```
